# Optimizing a Trainium2 kernel written in Bass

```python
import numpy as np
import jax
import jax.numpy as jnp

def _softmax(x, axis=-1):
    return jax.nn.softmax(x, axis=axis)

def _gelu(x):
    return jax.nn.gelu(x, approximate=True)

def _silu(x):
    return jax.nn.silu(x)

def _sigmoid(x):
    return jax.nn.sigmoid(x)

def _layernorm(x, axis=-1, eps=1e-05):
    m = jnp.mean(x, axis=axis, keepdims=True)
    v = jnp.var(x, axis=axis, keepdims=True)
    return (x - m) / jnp.sqrt(v + eps)

def _scatter_add(tgt, idx, src, axis=0):
    return tgt.at[idx].add(src)

def _segment_sum(src, seg, n):
    return jax.ops.segment_sum(src, seg, n)
kernel_name = 'mk_xattn_seq_d1_seqx_r2_432b35'

def setup_inputs(seed: int=0):
    np.random.seed(seed)
    _w = jnp.asarray

    def _rec_inputs():
        import jax
        import jax.numpy as jnp
        _rk = jax.random.key(seed)
        x = -0.0005207 + 1.001 * jax.random.normal(jax.random.fold_in(_rk, 1), (16, 256, 512), jnp.float32)
        _lenS = 256 - jax.random.randint(jax.random.fold_in(_rk, 7), (16,), 0, max(1, 256 // 4) + 1, jnp.int32)
        _lenS2 = 256 - jax.random.randint(jax.random.fold_in(_rk, 8), (16,), 0, max(1, 256 // 4) + 1, jnp.int32)
        _ctx_1024P = jax.random.normal(jax.random.fold_in(_rk, 11), (16, 16, 512), jnp.float32)
        _ctx_1024c = jax.random.dirichlet(jax.random.fold_in(_rk, 511), 0.3 * jnp.ones((16,), jnp.float32), (16, 256))
        _ctx_1024t = jnp.einsum('bsk,bkd->bsd', _ctx_1024c, _ctx_1024P)
        _ctx_1024t = _ctx_1024t * jax.lax.rsqrt(jnp.mean(jnp.square(_ctx_1024t)) + 1e-12) * 0.953939
        ctx_1024 = 4.13588e-05 + 0.999923 * (_ctx_1024t + 0.3 * jax.random.normal(jax.random.fold_in(_rk, 611), (16, 256, 512), jnp.float32))
        fside_BxSx2_0 = jax.random.uniform(jax.random.fold_in(_rk, 13), (16, 256, 2), jnp.float32, 0.0, 0.999707)
        fside_BxS2x2_0 = jax.random.uniform(jax.random.fold_in(_rk, 14), (16, 256, 2), jnp.float32, 0.0, 0.999884)
        _validS = jnp.arange(256)[None, :] < _lenS[:, None]
        _validS2 = jnp.arange(256)[None, :] < _lenS2[:, None]
        _causal = jnp.tril(jnp.ones((256, 256), dtype=bool))
        mask_BxS2_bf1 = jnp.ones((16, 256), dtype=bool)
        return (x, ctx_1024, fside_BxSx2_0, fside_BxS2x2_0, mask_BxS2_bf1)
    x, ctx_1024, fside_BxSx2_0, fside_BxS2x2_0, mask_BxS2_bf1 = _rec_inputs()

    def _L0_xattn_setup():
        import jax, jax.numpy as jnp
        import numpy as np
        LN_EPS = 1e-05

        def _ln(x, g, b):
            mu = jnp.mean(x, axis=-1, keepdims=True)
            var = jnp.var(x, axis=-1, keepdims=True)
            return (x - mu) * jax.lax.rsqrt(var + LN_EPS) * g + b
        key = jax.random.key(seed)
        ks = jax.random.split(key, 16)
        B, L, T, D, H = (4, 256, 1024, 512, 16)
        Dh = D * 4
        s = 0.02
        return {'queries': jax.random.normal(ks[0], (B, L, D), jnp.float32), 'tokens': jax.random.normal(ks[1], (B, T, D), jnp.float32), 'token_mask': jnp.ones((B, T), jnp.bool_), 'query_coords': jax.random.uniform(ks[2], (B, L, 2), jnp.float32), 'token_coords': jax.random.uniform(ks[3], (B, T, 2), jnp.float32), 'q_norm_g': jnp.ones((D,), jnp.float32), 'q_norm_b': jnp.zeros((D,), jnp.float32), 'kv_norm_g': jnp.ones((D,), jnp.float32), 'kv_norm_b': jnp.zeros((D,), jnp.float32), 'in_proj_w': jax.random.normal(ks[4], (3 * D, D), jnp.float32) * s, 'in_proj_b': jnp.zeros((3 * D,), jnp.float32), 'out_proj_w': jax.random.normal(ks[5], (D, D), jnp.float32) * s, 'out_proj_b': jnp.zeros((D,), jnp.float32), 'spatial_scale': jnp.ones((H,), jnp.float32), 'spatial_offset': jnp.zeros((H,), jnp.float32), 'mlp_norm_g': jnp.ones((D,), jnp.float32), 'mlp_norm_b': jnp.zeros((D,), jnp.float32), 'mlp_w1': jax.random.normal(ks[6], (Dh, D), jnp.float32) * s, 'mlp_b1': jnp.zeros((Dh,), jnp.float32), 'mlp_w2': jax.random.normal(ks[7], (D, Dh), jnp.float32) * s, 'mlp_b2': jnp.zeros((D,), jnp.float32)}
    _L0_xattn_all = _L0_xattn_setup()
    _L0_xattn_in = {k: v for k, v in _L0_xattn_all.items() if k in ('q_norm_g', 'q_norm_b', 'kv_norm_g', 'kv_norm_b', 'in_proj_w', 'in_proj_b', 'out_proj_w', 'out_proj_b', 'spatial_scale', 'spatial_offset', 'mlp_norm_g', 'mlp_norm_b', 'mlp_w1', 'mlp_b1', 'mlp_w2', 'mlp_b2')}
    del _L0_xattn_all
    return {'x': x, 'ctx_1024': ctx_1024, 'fside_BxSx2_0': fside_BxSx2_0, 'fside_BxS2x2_0': fside_BxS2x2_0, 'mask_BxS2_bf1': mask_BxS2_bf1, 'L0_xattn_q_norm_g': _L0_xattn_in['q_norm_g'], 'L0_xattn_q_norm_b': _L0_xattn_in['q_norm_b'], 'L0_xattn_kv_norm_g': _L0_xattn_in['kv_norm_g'], 'L0_xattn_kv_norm_b': _L0_xattn_in['kv_norm_b'], 'L0_xattn_in_proj_w': _L0_xattn_in['in_proj_w'], 'L0_xattn_in_proj_b': _L0_xattn_in['in_proj_b'], 'L0_xattn_out_proj_w': _L0_xattn_in['out_proj_w'], 'L0_xattn_out_proj_b': _L0_xattn_in['out_proj_b'], 'L0_xattn_spatial_scale': _L0_xattn_in['spatial_scale'], 'L0_xattn_spatial_offset': _L0_xattn_in['spatial_offset'], 'L0_xattn_mlp_norm_g': _L0_xattn_in['mlp_norm_g'], 'L0_xattn_mlp_norm_b': _L0_xattn_in['mlp_norm_b'], 'L0_xattn_mlp_w1': _L0_xattn_in['mlp_w1'], 'L0_xattn_mlp_b1': _L0_xattn_in['mlp_b1'], 'L0_xattn_mlp_w2': _L0_xattn_in['mlp_w2'], 'L0_xattn_mlp_b2': _L0_xattn_in['mlp_b2']}

def reference(x, ctx_1024, fside_BxSx2_0, fside_BxS2x2_0, mask_BxS2_bf1, L0_xattn_q_norm_g, L0_xattn_q_norm_b, L0_xattn_kv_norm_g, L0_xattn_kv_norm_b, L0_xattn_in_proj_w, L0_xattn_in_proj_b, L0_xattn_out_proj_w, L0_xattn_out_proj_b, L0_xattn_spatial_scale, L0_xattn_spatial_offset, L0_xattn_mlp_norm_g, L0_xattn_mlp_norm_b, L0_xattn_mlp_w1, L0_xattn_mlp_b1, L0_xattn_mlp_w2, L0_xattn_mlp_b2):
    import jax
    import jax.numpy as jnp

    def _L0_xattn_ref(queries, tokens, token_mask, query_coords, token_coords, q_norm_g, q_norm_b, kv_norm_g, kv_norm_b, in_proj_w, in_proj_b, out_proj_w, out_proj_b, spatial_scale, spatial_offset, mlp_norm_g, mlp_norm_b, mlp_w1, mlp_b1, mlp_w2, mlp_b2):
        import jax, jax.numpy as jnp
        import numpy as np
        LN_EPS = 1e-05

        def _ln(x, g, b):
            mu = jnp.mean(x, axis=-1, keepdims=True)
            var = jnp.var(x, axis=-1, keepdims=True)
            return (x - mu) * jax.lax.rsqrt(var + LN_EPS) * g + b
        B, L, D = queries.shape
        T = tokens.shape[1]
        H = spatial_scale.shape[0]
        hd = D // H
        q = _ln(queries, q_norm_g, q_norm_b)
        kv = _ln(tokens, kv_norm_g, kv_norm_b)
        qp = q @ in_proj_w[:D].T + in_proj_b[:D]
        kp = kv @ in_proj_w[D:2 * D].T + in_proj_b[D:2 * D]
        vp = kv @ in_proj_w[2 * D:].T + in_proj_b[2 * D:]
        qh = qp.reshape(B, L, H, hd).transpose(0, 2, 1, 3)
        kh = kp.reshape(B, T, H, hd).transpose(0, 2, 1, 3)
        vh = vp.reshape(B, T, H, hd).transpose(0, 2, 1, 3)
        scores = jnp.einsum('bhld,bhtd->bhlt', qh, kh) / np.sqrt(hd).astype(np.float32)
        diff = query_coords[:, :, None, :] - token_coords[:, None, :, :]
        dist = jnp.sqrt(jnp.maximum(jnp.sum(diff * diff, axis=-1), 0.0))
        bias = -spatial_scale[None, :, None, None] * dist[:, None] + spatial_offset[None, :, None, None]
        scores = scores + bias
        key_padding = ~token_mask
        scores = jnp.where(key_padding[:, None, None, :], -jnp.inf, scores)
        attn = jax.nn.softmax(scores, axis=-1)
        attn_out = jnp.einsum('bhlt,bhtd->bhld', attn, vh)
        attn_out = attn_out.transpose(0, 2, 1, 3).reshape(B, L, D)
        attn_out = attn_out @ out_proj_w.T + out_proj_b
        x = queries + attn_out
        h = _ln(x, mlp_norm_g, mlp_norm_b)
        h = jax.nn.gelu(h @ mlp_w1.T + mlp_b1, approximate=False)
        x = x + (h @ mlp_w2.T + mlp_b2)
        return x
    x = _L0_xattn_ref(x, ctx_1024, mask_BxS2_bf1, fside_BxSx2_0, fside_BxS2x2_0, L0_xattn_q_norm_g, L0_xattn_q_norm_b, L0_xattn_kv_norm_g, L0_xattn_kv_norm_b, L0_xattn_in_proj_w, L0_xattn_in_proj_b, L0_xattn_out_proj_w, L0_xattn_out_proj_b, L0_xattn_spatial_scale, L0_xattn_spatial_offset, L0_xattn_mlp_norm_g, L0_xattn_mlp_norm_b, L0_xattn_mlp_w1, L0_xattn_mlp_b1, L0_xattn_mlp_w2, L0_xattn_mlp_b2)
    return x

_drawn_inputs = setup_inputs


def setup_inputs(seed=0):
    import zlib

    import numpy as np

    out = dict(_drawn_inputs(seed))
    spreads = {'L0_xattn_q_norm_g': (1.0, 0.6),
     'L0_xattn_q_norm_b': (0.0, 2.0),
     'L0_xattn_kv_norm_g': (1.0, 0.6),
     'L0_xattn_kv_norm_b': (0.0, 0.42),
     'L0_xattn_in_proj_b': (0.0, 0.1),
     'L0_xattn_out_proj_b': (0.0, 0.1),
     'L0_xattn_spatial_scale': (1.0, 0.6),
     'L0_xattn_spatial_offset': (0.0, 2.0),
     'L0_xattn_mlp_norm_g': (1.0, 0.2),
     'L0_xattn_mlp_norm_b': (0.0, 0.348),
     'L0_xattn_mlp_b1': (0.0, 0.1),
     'L0_xattn_mlp_b2': (0.0, 0.1)}
    factors = {'fside_BxSx2_0': 8.0, 'fside_BxS2x2_0': 8.0}
    for name, (base, spread) in spreads.items():
        noise = np.random.default_rng([zlib.crc32(name.encode()), seed]).standard_normal(out[name].shape)
        drawn = base * np.exp(spread * noise) if base else spread * noise
        out[name] = jnp.asarray(drawn.astype(out[name].dtype))
    for name, factor in factors.items():
        out[name] = (out[name] * factor).astype(out[name].dtype)
    return out
```

```python
from contextlib import ExitStack

import concourse.bass as bass
from concourse import mybir

F32 = mybir.dt.float32
F32R = mybir.dt.float32r
BF16 = mybir.dt.bfloat16
F16 = mybir.dt.float16
U8 = mybir.dt.uint8
ALU = mybir.AluOpType
ACT = mybir.ActivationFunctionType

P = 128
LN_EPS = 1e-05
P_SCALE = 2.0 ** 14
HI, LO = 0, 1
PASSES = ((HI, HI), (HI, LO), (LO, HI))
PV_PASSES = ((0, 0), (0, 1), (0, 2), (1, 0), (1, 1))


class Signal:

    def __init__(self, sem, step=1):
        self.sem, self.step, self.count = sem, step, 0


class Queue:

    def __init__(self):
        self.ops, self.seen = [], {}

    def wait(self, *marks):
        for mark in marks:
            if mark is None:
                continue
            signal, value = mark
            if self.seen.get(id(signal), 0) < value:
                self.seen[id(signal)] = value
                self.ops.append(lambda e, s=signal.sem, v=value: e.wait_ge(s, v))

    def do(self, make, signal=None):
        if signal is None:
            self.ops.append(make)
            return None
        signal.count += signal.step
        self.ops.append(lambda e, s=signal: make(e).then_inc(s.sem, s.step))
        return signal, signal.count

    def run(self, engine):
        for op in self.ops:
            op(engine)


def build_block(nc, x, ctx, tok_xy, q_xy, mask, w_qkv, w_o, w_1, w_2, cols, b_o, b_2, sp_scale, sp_offset, out, x1_dram):
    B, L, D = x.shape
    T = ctx.shape[1]
    H = sp_scale.shape[1]
    HD = D // H
    FF = w_1.shape[1]
    KT = D // P
    LC, TC = L // P, T // P
    HG, HPG = H // 4, 4
    MT = FF // P
    N_ITEMS = B * H
    GROUP_TOK = 512
    N_GROUPS = B * L // GROUP_TOK
    GT = GROUP_TOK // P
    SCORE_SCALE = float(HD) ** -0.5
    assert (L, T, D, HD, KT, HG) == (256, 256, 512, 32, 4, 4)

    es = ExitStack()
    with es:
        ARENA = 16512
        top = [ARENA]

        def sb(name, shape, dt, at=None):
            size = mybir.dt.size(dt)
            for s in shape[1:]:
                size *= s
            off = top[0] if at is None else at
            if at is None:
                top[0] += (size + 31) // 32 * 32
                assert top[0] <= 229344, (name, top[0])
            return nc.alloc_sbuf_tensor_at(name, shape, dt, offset=off)

        ident = sb("ident", [P, P], F32)
        cols_sb = sb("cols", [P, cols.shape[1]], F32)
        scale_neg = sb("scale_neg", [P, H], F32)
        offset_sb = sb("offset", [P, H], F32)
        q_neg = sb("q_neg", [P, B * LC * 2], F32)
        gq = sb("gq", [P, KT], F32)
        bias_qkv = sb("bias_qkv", [P, 12], F32)
        bias_1 = sb("bias_1", [P, MT], F32)
        neg_half = sb("neg_half", [P, 4], F32)
        stats = sb("stats", [P, 4, 6], F32)
        mean_var = sb("mean_var", [P, 4, 2], F32)
        var_eps = sb("var_eps", [P, 4], F32)
        rstd = sb("rstd", [P, 4], F32)
        phase1 = top[0]
        b_o_sb = sb("b_o", [P, D], F32)
        neg_max = sb("neg_max", [P, 4, LC], F32)
        row_sum = sb("row_sum", [P, 4, LC], F32)
        row_inv = sb("row_inv", [P, 4, LC], F32)
        w_qkv_sb = sb("w_qkv_sb", [P, 2, KT, 3 * D], F32R)
        w_o_sb = sb("w_o_sb", [P, 2, KT, D], F32R)
        xT = sb("xT", [P, 2, 2, 2, KT, L], F32R)
        stack = sb("stack", [P, 4, 2, HPG, L], F32R)
        qk_parts = sb("qk_parts", [P, 2, 2, L], F32R)
        v_parts = sb("v_parts", [P, 2, TC, 3, D], BF16)
        v_rest = sb("v_rest", [P, D], F32)
        attnT = sb("attnT", [P, 2, 2, HG, L], F32R)
        attn_y = sb("attn_y", [P, L], F32)
        raw = sb("raw", [P, 4, D], F32)
        x1_t = sb("x1_t", [P, 2, D], F32)
        dist = sb("dist", [P, 2, LC, T], F32)
        tok_rows = sb("tok_rows", [P, 2, T], F32)
        sq = sb("sq", [P, 2, LC, T], F32)
        mask_u8 = sb("mask_u8", [P, T], U8)
        mask_row = sb("mask_row", [P, T], F32)
        soft = sb("soft", [P, 4, LC, T], F32)
        PT_RING = 5
        pT = sb("pT", [P, PT_RING, 2, TC * L], F16)

        top[0] = phase1
        w_1_sb = sb("w_1_sb", [P, 2, KT, FF], F32R)
        w_2_sb = sb("w_2_sb", [P, 2, MT, D], F32R)
        hT = sb("hT", [P, 2, 2, KT, GROUP_TOK], F32R)
        hid = sb("hid", [P, 3, 2, GROUP_TOK], F32R)
        gelu = sb("gelu", [P, 2, GROUP_TOK], F32)
        x1_g = sb("x1_g", [P, 2, GT, D], F32)
        x1_n = sb("x1_n", [P, 2, D], F32)
        b_2_sb = sb("b_2", [P, D], F32)
        hT1_at = phase1 + 2 * 2 * 4 * KT * FF // 1 * 0
        w_stage = sb("w_stage", [P, 8, D], F32, at=phase1 + (2 * KT * FF + 2 * MT * D + 2 * KT * GROUP_TOK) * 4)

        def bank(name):
            return es.enter_context(nc.psum_tensor(name, [P, 512], F32))

        ps_s = [bank("ps_s0"), bank("ps_s1")]
        ps_pt = [bank("ps_pt0"), bank("ps_pt1")]
        ps_pv = bank("ps_pv")
        ps_tr = bank("ps_tr")
        ps_qk = bank("ps_qk")
        ps_vo = bank("ps_vo")

        def sig(name, step=1):
            return Signal(es.enter_context(nc.semaphore(name)), step)

        def dsig(name):
            return sig(name, 16)

        pe, act, dve, pool, sp = Queue(), Queue(), Queue(), Queue(), Queue()

        s_cols, s_small, s_bo = dsig("s_cols"), dsig("s_small"), dsig("s_bo")
        cols_in = sp.do(lambda e: e.dma_start(cols_sb[:], cols), s_cols)
        small_in = None
        for dst, src in ((scale_neg[:], sp_scale.to_broadcast([P, H])), (offset_sb[:], sp_offset.to_broadcast([P, H])),
                         (q_neg[:], q_xy)):
            small_in = sp.do(lambda e, d=dst, s=src: e.dma_start(d, s), s_small)
        G_Q, B_Q, G_KV, B_KV, B_IN, G_M, B_M, B_1 = 0, 4, 8, 12, 16, 28, 32, 36

        s_id, s_cst = sig("s_id"), sig("s_cst")
        pool.wait(pool.do(lambda e: e.memset(ident[:], 0.0), s_id))
        ident_done = pool.do(lambda e: e.affine_select(out=ident[:], in_=ident[:], compare_op=ALU.not_equal, fill=1.0,
                                                       base=0, pattern=[[-1, P]], channel_multiplier=1), s_id)
        pool.wait(ident_done)
        ones_done = pool.do(lambda e: e.memset(stack[96:97, :, 0, :, :].bitcast(F32), 1.0), s_id)
        pool.wait(ones_done)
        half_done = pool.do(lambda e: e.memset(neg_half[:], -0.5), s_id)
        dve.wait(cols_in, small_in)
        dve.do(lambda e: e.tensor_scalar(scale_neg[:], scale_neg[:], -1.0, None, ALU.mult), s_cst)
        gq_done = dve.do(lambda e: e.tensor_scalar(gq[:], cols_sb[:, G_Q:G_Q + KT], SCORE_SCALE, None, ALU.mult), s_cst)
        consts_done = dve.do(lambda e: e.tensor_scalar(q_neg[:], q_neg[:], -1.0, None, ALU.mult), s_cst)

        s_w = [dsig("s_w0"), dsig("s_w1")]
        s_w_hi, s_w_lo, s_bmm, s_bcol = sig("s_w_hi"), sig("s_w_lo"), sig("s_bmm"), sig("s_bcol")
        stages = (raw[:], soft[:].rearrange("p a b c -> p a (b c)"))
        w_lo_done = {}
        bmm_done = None

        def weight_parts(sec, k):
            if sec < 3:
                return [w_qkv_sb[:, part, k, sec * D:(sec + 1) * D] for part in (HI, LO)]
            return [w_o_sb[:, part, k, :] for part in (HI, LO)]

        for sec in range(4):
            stage = stages[sec % 2]
            src = w_o if sec == 3 else w_qkv[:, sec * D:(sec + 1) * D]
            sp.wait(w_lo_done.get(sec - 2), bmm_done if sec >= 2 else None)
            w_in = sp.do(lambda e, d=stage, s=src.rearrange("(k p) n -> p k n", p=P): e.dma_start(d, s), s_w[sec % 2])
            if sec < 3:
                b_ln = B_Q if sec == 0 else B_KV
                pe.wait(w_in, cols_in)
                for m in range(KT):
                    for k in range(KT):
                        mm = lambda e, m=m, k=k, sec=sec, st=stage, b=b_ln: e.matmul(
                            ps_tr[:, sec * KT + m:sec * KT + m + 1], st[:, k, m * P:(m + 1) * P],
                            cols_sb[:, b + k:b + k + 1], start=(k == 0), stop=(k == KT - 1))
                        last = pe.do(mm, s_bmm if (m, k) == (KT - 1, KT - 1) else None)
                bmm_done = last
            act.wait(w_in, gq_done)
            dve.wait(w_in)
            for k in range(KT):
                hi, lo = weight_parts(sec, k)
                g = {0: gq[:, k:k + 1], 3: 1.0}.get(sec, cols_sb[:, G_KV + k:G_KV + k + 1])
                hi_done = act.do(lambda e, o=hi, i=stage[:, k, :], g=g: e.activation(o, i, ACT.Copy, scale=g), s_w_hi)
                dve.wait(hi_done, gq_done)
                w_lo_done[sec] = dve.do(lambda e, o=lo, i=stage[:, k, :], g=g, h=hi: e.scalar_tensor_tensor(
                    out=o, in0=i, scalar=g, in1=h.bitcast(F32), op0=ALU.mult, op1=ALU.subtract), s_w_lo)
        stage_free = (w_lo_done[3], w_lo_done[2], bmm_done)
        bo_in = sp.do(lambda e: e.dma_start(b_o_sb[:], b_o.to_broadcast([P, D])), s_bo)
        dve.wait(bmm_done)
        dve.wait(dve.do(lambda e: e.tensor_tensor(bias_qkv[:], ps_tr[:, 0:12], cols_sb[:, B_IN:B_IN + 12], ALU.add), s_bcol))
        bcol_done = dve.do(lambda e: e.tensor_scalar(bias_qkv[:, 0:KT], bias_qkv[:, 0:KT], SCORE_SCALE, None, ALU.mult), s_bcol)

        s_raw = [dsig(f"s_raw{i}") for i in range(4)]
        s_st, s_ag, s_ve, s_rs, s_ap = sig("s_st"), sig("s_ag"), sig("s_ve"), sig("s_rs"), sig("s_ap")
        s_xtr, s_xhi, s_xlo = sig("s_xtr"), sig("s_xhi"), sig("s_xlo")
        s_qk, s_qkhi, s_qklo = sig("s_qk"), sig("s_qkhi"), sig("s_qklo")
        s_stack = [dsig(f"s_stack{i}") for i in range(4)]
        s_v, s_va, s_vr, s_vb, s_vr2, s_vc = [sig(n) for n in ("s_v", "s_va", "s_vr", "s_vb", "s_vr2", "s_vc")]
        s_xy, s_sq, s_d2, s_dist = dsig("s_xy"), sig("s_sq"), sig("s_d2"), sig("s_dist")
        s_mu, s_mrow = dsig("s_mu"), sig("s_mrow")
        s_bias, s_score, s_max, s_exp, s_inv, s_norm = [sig(n) for n in ("s_bias", "s_score", "s_max", "s_exp", "s_inv", "s_norm")]
        s_t, s_pthi, s_ptlo, s_pv, s_y, s_ahi, s_alo = [sig(n) for n in ("s_t", "s_pthi", "s_ptlo", "s_pv", "s_y", "s_ahi", "s_alo")]
        s_o, s_res, s_resb, s_x1 = sig("s_o"), [dsig("s_res0"), dsig("s_res1")], sig("s_resb"), sig("s_x1")
        s_x1st = [dsig("s_x1st0"), dsig("s_x1st1")]
        done = {}
        FIRST_USE = ("xlo_last", "qklo_last", "vo_free", "vc_last", "glo_last")

        def got(*key):
            if key not in done and (key[0] in FIRST_USE or any(i < 0 for i in key[1:])):
                return None
            return done[key]

        x_rows = x.rearrange("b (c p) d -> (b c) p d", p=P)
        c_rows = ctx.rearrange("b (c p) d -> (b c) p d", p=P)

        def load_inputs(b):
            for i in range(4):
                src = (x_rows if i < 2 else c_rows)[b * 2 + i % 2]
                sp.wait(got("xtr", b - 1, i), *(stage_free if b == 0 else ()))
                done["raw", b, i] = sp.do(lambda e, i=i, s=src: e.dma_start(raw[:, i, :], s), s_raw[i])

        def load_geometry(b):
            sp.wait(got("sq", b - 1))
            done["xy", b] = sp.do(lambda e, b=b: e.dma_start(
                tok_rows[:], tok_xy[b:b + 1].to_broadcast([P, 2, T])), s_xy)
            sp.wait(got("mrow_conv", b - 1))
            done["mask", b] = sp.do(lambda e, b=b: e.dma_start(mask_u8[96:97, :], mask[b:b + 1, :]), s_mu)

        def norm_stats(b, i):
            dve.wait(got("raw", b, i), got("ap", b - 1, 3))
            st = dve.do(lambda e, i=i: e.bn_stats(stats[:, i, :], raw[:, i, :]), s_st)
            dve.wait(st)
            done["ag", b] = dve.do(lambda e, i=i: e.bn_aggr(mean_var[:, i, :], stats[:, i, :]), s_ag)

        def norm_rstd(b):
            dve.wait(got("ag", b))
            ve = dve.do(lambda e: e.tensor_scalar(var_eps[:], mean_var[:, :, 1], LN_EPS, None, ALU.add), s_ve)
            pool.wait(ve, half_done)
            done["rstd", b] = pool.do(lambda e: e.tensor_tensor(rstd[:], var_eps[:], neg_half[:], ALU.pow), s_rs)

        def norm_apply(b, i):
            dve.wait(got("rstd", b))
            done["ap", b, i] = dve.do(lambda e, i=i: e.tensor_scalar(
                raw[:, i, :], raw[:, i, :], mean_var[:, i, 0:1], rstd[:, i:i + 1], ALU.subtract, ALU.mult), s_ap)

        def x_transpose(b, i):
            pe.wait(got("ap", b, i), got("xlo_last"), ident_done, bcol_done)
            for k in range(KT):
                tr = lambda e, i=i, k=k: e.transpose(ps_tr[:, k * P:(k + 1) * P], raw[:, i, k * P:(k + 1) * P], ident[:])
                last = pe.do(tr, s_xtr if k == KT - 1 else None)
            done["xtr", b, i] = last

        def x_parts(b, i):
            ring, which, tok = b % 2, i // 2, (i % 2) * P
            src = ps_tr[:].rearrange("p (k t) -> p k t", k=KT)
            hi = xT[:, ring, which, HI, :, tok:tok + P]
            lo = xT[:, ring, which, LO, :, tok:tok + P]
            act.wait(got("xtr", b, i), got("qk", 4 * (b - 2) + 3, 1), got("vproj", b - 2, 1))
            hi_done = act.do(lambda e, o=hi, s=src: e.activation(o, s, ACT.Copy), s_xhi)
            dve.wait(hi_done)
            done["xlo", b, i] = done["xlo_last",] = dve.do(lambda e, o=lo, s=src, h=hi: e.tensor_tensor(
                o, s, h.bitcast(F32), ALU.subtract), s_xlo)

        def qk_steps(G, which):
            b, hg = divmod(G, HG)
            ring = b % 2
            steps = []
            for k in range(KT):
                for wp, xp in PASSES:
                    first, last = (k, wp, xp) == (0, 0, 0), (k, wp, xp) == (KT - 1,) + PASSES[-1]
                    col = which * D + hg * P
                    mm = lambda e, k=k, wp=wp, xp=xp, f=first, l=last, c=col: e.matmul(
                        ps_qk[:, 0:L], w_qkv_sb[:, wp, k, c:c + P], xT[:, ring, which, xp, k, :], start=f, stop=l)

                    def step(mm=mm, f=first, l=last):
                        if f:
                            pe.wait(got("xlo", b, 2 * which + 1), got("qklo_last"), w_lo_done[which])
                        r = pe.do(mm, s_qk if l else None)
                        if l:
                            done["qk", G, which] = r
                    steps.append(step)
            return steps

        def qk_split(G, which):
            b, hg = divmod(G, HG)
            hi, lo = qk_parts[:, which, HI, :], qk_parts[:, which, LO, :]
            col = bias_qkv[:, which * KT + hg:which * KT + hg + 1]
            act.wait(got("qk", G, which), got("stack", G - 1), bcol_done)
            hi_done = act.do(lambda e, o=hi, c=col: e.activation(o, ps_qk[:, 0:L], ACT.Identity, bias=c), s_qkhi)
            dve.wait(hi_done)
            done["qklo", G, which] = done["qklo_last",] = dve.do(lambda e, o=lo, h=hi, c=col: e.scalar_tensor_tensor(
                out=o, in0=ps_qk[:, 0:L], scalar=c, in1=h.bitcast(F32), op0=ALU.add, op1=ALU.subtract), s_qklo)

        def stack_copies(G):
            b, hg = divmod(G, HG)
            slot = G % 4
            sp.wait(got("qklo", G, 0), got("qklo", G, 1), got("score", 4 * (G - 4) + 3), got("mrow", b), ones_done)
            for j in range(HPG):
                for r, (qp, kp) in enumerate(PASSES_QK):
                    base = qk_parts[32 * j:32 * j + 32, :, :, :].bitcast(F32).rearrange("p w s l -> p (w s) l")
                    src = base[:, qp:kp + 3:kp + 2 - qp, :]
                    dst = stack[32 * r:32 * r + 32, slot, :, j, :].bitcast(F32)
                    sp.do(lambda e, d=dst, s=src: e.dma_start(d, s), s_stack[slot])
            dst = stack[96:97, slot, 1, :, :].bitcast(F32)
            src = mask_row[96:97, :].rearrange("p (o t) -> p o t", o=1).to_broadcast([1, HPG, T])
            done["stack", G] = sp.do(lambda e, d=dst, s=src: e.dma_start(d, s), s_stack[slot])

        PASSES_QK = ((HI, HI), (HI, LO), (LO, HI))

        def mask_steps(b):
            row, src = mask_row[96:97, :], mask_u8[96:97, :]
            dve.wait(got("mask", b), got("stack", 4 * b - 1))
            m1 = dve.do(lambda e: e.tensor_scalar(row, src, 0.0, -3.0e38, ALU.is_equal, ALU.mult), s_mrow)
            done["mrow_conv", b] = m1
            dve.wait(m1)
            done["mrow", b] = dve.do(lambda e: e.tensor_scalar(row, row, 3.0e38, None, ALU.mult), s_mrow)

        def v_steps(b, tt):
            ring = b % 2
            steps = []
            for k in range(KT):
                for xp, wp in PASSES:
                    first, last = (k, xp, wp) == (0, 0, 0), (k, xp, wp) == (KT - 1,) + PASSES[-1]
                    mm = lambda e, k=k, wp=wp, xp=xp, f=first, l=last: e.matmul(
                        ps_vo[:], xT[:, ring, 1, xp, k, tt * P:(tt + 1) * P], w_qkv_sb[:, wp, k, 2 * D:3 * D], start=f, stop=l)

                    def step(mm=mm, f=first, l=last):
                        if f:
                            pe.wait(got("xlo", b, 3), got("vo_free"), w_lo_done[2])
                        r = pe.do(mm, s_v if l else None)
                        if l:
                            done["vproj", b, tt] = r
                    steps.append(step)
            return steps

        def v_split(b, tt):
            a, m, c = [v_parts[:, b % 2, tt, part, :] for part in range(3)]
            act.wait(got("vproj", b, tt), got("pv", 4 * (b - 2) + 3))
            va = act.do(lambda e: e.activation(a, ps_vo[:], ACT.Copy), s_va)
            dve.wait(va, got("vc_last"))
            r1 = done["vo_free",] = dve.do(lambda e: e.tensor_tensor(v_rest[:], ps_vo[:], a, ALU.subtract), s_vr)
            act.wait(r1)
            vb = act.do(lambda e: e.activation(m, v_rest[:], ACT.Copy), s_vb)
            pool.wait(r1, vb)
            done["v", b, tt] = done["vc_last",] = pool.do(lambda e: e.tensor_tensor(c, v_rest[:], m, ALU.subtract), s_vc)

        def dist_squares(b):
            act.wait(got("xy", b), consts_done, got("d2", b - 1))
            for c in range(2):
                for lc in range(LC):
                    col = (b * LC + lc) * 2 + c
                    done["sq", b] = act.do(lambda e, c=c, lc=lc, col=col: e.activation(
                        sq[:, c, lc, :], tok_rows[:, c, :], ACT.Square, bias=q_neg[:, col:col + 1]), s_sq)

        def dist_sum(b):
            dve.wait(got("sq", b), got("dist", b - 1))
            d2 = dve.do(lambda e: e.tensor_tensor(sq[:, 0, :, :], sq[:, 0, :, :], sq[:, 1, :, :], ALU.add), s_d2)
            dve.wait(d2)
            done["d2max", b] = dve.do(lambda e: e.tensor_scalar(sq[:, 0, :, :], sq[:, 0, :, :], 0.0, None, ALU.max), s_d2)

        def dist_sqrt(b):
            act.wait(got("d2max", b), got("bias", H * (b - 1) - 1))
            done["dist", b] = done["d2", b] = act.do(lambda e, b=b: e.activation(
                dist[:, b % 2, :, :], sq[:, 0, :, :], ACT.Sqrt), s_dist)

        def bias_tile(i):
            b, h = divmod(i, H)
            pool.wait(got("dist", b), got("t", i - 4), consts_done, *(stage_free if i < 4 else ()))
            done["bias", i] = pool.do(lambda e: e.tensor_scalar(
                soft[:, i % 4, :, :], dist[:, b % 2, :, :], scale_neg[:, h:h + 1], offset_sb[:, h:h + 1], ALU.mult, ALU.add), s_bias)

        def scores(i):
            b, h = divmod(i, H)
            slot, j = (i // 4) % 4, i % 4
            pe.wait(got("stack", i // 4), got("max", i - 2))
            for lc in range(LC):
                mm = lambda e, lc=lc: e.matmul(ps_s[i % 2][:, lc * T:(lc + 1) * T], stack[0:97, slot, 0, j, lc * P:(lc + 1) * P],
                                               stack[0:97, slot, 1, j, :], start=True, stop=True)
                r = pe.do(mm, s_score if lc == LC - 1 else None)
            done["score", i] = r

        def score_max(i):
            dve.wait(got("score", i), got("bias", i), got("exp", i - 4))
            for lc in range(LC):
                done["max", i] = done["max", i, lc] = dve.do(lambda e, lc=lc: e.tensor_tensor_reduce(
                    soft[:, i % 4, lc, :], ps_s[i % 2][:, lc * T:(lc + 1) * T], soft[:, i % 4, lc, :], -1.0, 3.0e38,
                    ALU.add, ALU.min, neg_max[:, i % 4, lc:lc + 1]), s_max)

        def exps(i):
            act.wait(got("inv", i - 4))
            for lc in range(LC):
                act.wait(got("max", i, lc))
                done["exp", i] = act.do(lambda e, lc=lc: e.activation(
                    soft[:, i % 4, lc, :], soft[:, i % 4, lc, :], ACT.Exp, scale=-1.0, bias=neg_max[:, i % 4, lc:lc + 1],
                    accum_out=row_sum[:, i % 4, lc:lc + 1]), s_exp)

        def inverse(i):
            dve.wait(got("exp", i), got("norm", i - 4))
            done["inv", i] = dve.do(lambda e: e.reciprocal(row_inv[:, i % 4, :], row_sum[:, i % 4, :]), s_inv)

        def normalise(i):
            pool.wait(got("inv", i))
            for lc in range(LC):
                done["norm", i] = pool.do(lambda e, lc=lc: e.tensor_scalar(
                    soft[:, i % 4, lc, :], soft[:, i % 4, lc, :], row_inv[:, i % 4, lc:lc + 1], P_SCALE, ALU.mult, ALU.mult), s_norm)

        def p_transpose(i):
            pe.wait(got("norm", i), got("ptlo", i - 2))
            for tc in range(TC):
                for lc in range(LC):
                    tr = lambda e, tc=tc, lc=lc: e.transpose(
                        ps_pt[i % 2][:, tc * L + lc * P:tc * L + (lc + 1) * P], soft[:, i % 4, lc, tc * P:(tc + 1) * P], ident[:])
                    r = pe.do(tr, s_t if (tc, lc) == (TC - 1, LC - 1) else None)
            done["t", i] = r

        def p_parts(i):
            hi, lo = pT[:, i % PT_RING, 0, :], pT[:, i % PT_RING, 1, :]
            act.wait(got("t", i), got("pv", (i - PT_RING) // 4) if i >= PT_RING else None)
            hi_done = act.do(lambda e: e.activation(hi, ps_pt[i % 2][:], ACT.Copy), s_pthi)
            dve.wait(hi_done)
            done["ptlo", i] = dve.do(lambda e: e.tensor_tensor(lo, ps_pt[i % 2][:], hi, ALU.subtract), s_ptlo)

        def attend(G):
            b, hg = divmod(G, HG)
            pe.wait(got("ptlo", 4 * G + 3), got("v", b, 1), got("y", G - 1))
            n = 0
            for tc in range(TC):
                for pp, vp in PV_PASSES:
                    for j in range(HPG):
                        h = hg * HPG + j
                        mm = lambda e, tc=tc, pp=pp, vp=vp, j=j, h=h, n=n: e.matmul(
                            ps_pv[32 * j:32 * j + 32, 0:L], v_parts[:, b % 2, tc, vp, h * HD:(h + 1) * HD],
                            pT[:, (4 * G + j) % PT_RING, pp, tc * L:(tc + 1) * L],
                            start=(n == 0), stop=(n == TC * len(PV_PASSES) - 1))
                        r = pe.do(mm, s_pv if (n, j) == (TC * len(PV_PASSES) - 1, HPG - 1) else None)
                    n += 1
            done["pv", G] = r

        def attn_parts(G):
            b, hg = divmod(G, HG)
            hi, lo = attnT[:, b % 2, HI, hg, :], attnT[:, b % 2, LO, hg, :]
            dve.wait(got("pv", G), got("alo", G - 1), bcol_done)
            y = done["y", G] = dve.do(lambda e: e.tensor_scalar(
                attn_y[:], ps_pv[:, 0:L], 1.0 / P_SCALE, bias_qkv[:, 2 * KT + hg:2 * KT + hg + 1], ALU.mult, ALU.add), s_y)
            act.wait(y, got("oproj", b - 2, 1))
            hi_done = act.do(lambda e: e.activation(hi, attn_y[:], ACT.Copy), s_ahi)
            pool.wait(hi_done)
            done["alo", G] = pool.do(lambda e: e.tensor_tensor(lo, attn_y[:], hi.bitcast(F32), ALU.subtract), s_alo)

        def o_steps(b, tt):
            steps = []
            for k in range(KT):
                for ap_, wp in PASSES:
                    first, last = (k, ap_, wp) == (0, 0, 0), (k, ap_, wp) == (KT - 1,) + PASSES[-1]
                    mm = lambda e, k=k, wp=wp, ap_=ap_, f=first, l=last: e.matmul(
                        ps_vo[:], attnT[:, b % 2, ap_, k, tt * P:(tt + 1) * P], w_o_sb[:, wp, k, :], start=f, stop=l)

                    def step(mm=mm, f=first, l=last):
                        if f:
                            pe.wait(got("alo", 4 * b + 3), got("vo_free"), w_lo_done[3])
                        r = pe.do(mm, s_o if l else None)
                        if l:
                            done["oproj", b, tt] = r
                    steps.append(step)
            return steps

        def load_residual(b, tt):
            sp.wait(got("x1st", b - 1, tt))
            r = sp.do(lambda e: e.dma_start(x1_t[:, tt, :], x_rows[b * 2 + tt]), s_res[tt])
            pool.wait(r, bo_in)
            done["res", b, tt] = pool.do(lambda e: e.tensor_tensor(x1_t[:, tt, :], x1_t[:, tt, :], b_o_sb[:], ALU.add), s_resb)

        def add_residual(b, tt):
            dve.wait(got("oproj", b, tt), got("res", b, tt))
            r = done["vo_free",] = dve.do(lambda e: e.tensor_tensor(x1_t[:, tt, :], ps_vo[:], x1_t[:, tt, :], ALU.add), s_x1)
            sp.wait(r)
            done["x1st", b, tt] = sp.do(lambda e: e.dma_start(x1_dram[b * 2 + tt], x1_t[:, tt, :]), s_x1st[tt])

        load_inputs(0)
        load_geometry(0)
        for i in range(4):
            norm_stats(0, i)
        norm_rstd(0)
        for i in range(4):
            norm_apply(0, i)
            x_transpose(0, i)
            x_parts(0, i)
        dist_squares(0)
        dist_sum(0)
        dist_sqrt(0)
        mask_steps(0)
        load_inputs(1)
        load_geometry(1)
        for G in range(3):
            for which in range(2):
                for step in qk_steps(G, which):
                    step()
                qk_split(G, which)
            stack_copies(G)
        bias_tile(0)
        for tt in range(TC):
            for step in v_steps(0, tt):
                step()
            v_split(0, tt)
        for i in range(4):
            norm_stats(1, i)
        norm_rstd(1)
        for i in range(4):
            norm_apply(1, i)

        fill_vo, fill_qk = [], []
        for n in range(N_ITEMS + 10):
            b, h = divmod(n, H)
            G, j = divmod(n, 4)
            if h in (4, 7) and 0 < b <= B:
                fill_vo += o_steps(b - 1, (h - 4) // 3)
            if h in (10, 13) and b + 1 < B:
                fill_vo += v_steps(b + 1, (h - 10) // 3)
            if j in (0, 2) and G + 3 < B * HG:
                fill_qk += qk_steps(G + 3, j // 2)

            if n < N_ITEMS:
                scores(n)
                score_max(n)
                exps(n)
            for step in fill_vo[:4]:
                step()
            fill_vo = fill_vo[4:]
            if 0 <= n - 2 < N_ITEMS:
                p_transpose(n - 2)
            if j == 2 and G >= 1 and G - 1 < B * HG:
                attend(G - 1)
            if h in (6, 9) and 0 < b <= B:
                add_residual(b - 1, (h - 6) // 3)
            if 0 <= n - 2 < N_ITEMS:
                p_parts(n - 2)
            if n < N_ITEMS:
                inverse(n)
            if 0 <= n - 1 < N_ITEMS:
                normalise(n - 1)
            if n + 1 < N_ITEMS:
                bias_tile(n + 1)
            if j == 2 and G >= 1 and G - 1 < B * HG:
                attn_parts(G - 1)
            if h in (12, 15) and b + 1 < B:
                v_split(b + 1, (h - 12) // 3)
            for step in fill_qk[:6]:
                step()
            fill_qk = fill_qk[6:]
            if h < 4 and b + 1 < B:
                x_transpose(b + 1, h)
                x_parts(b + 1, h)
            if j in (1, 3) and G + 3 < B * HG:
                qk_split(G + 3, j // 2)
                if j == 3:
                    stack_copies(G + 3)
            if h == 0 and b < B:
                for tt in range(LC):
                    load_residual(b, tt) if b == 0 else None
            if h == 10 and 0 < b < B:
                for tt in range(LC):
                    load_residual(b, tt)
            if h == 4 and b + 1 < B:
                mask_steps(b + 1)
            if h == 4 and b + 2 < B:
                load_inputs(b + 2)
            if 6 <= h < 10 and b + 2 < B:
                norm_stats(b + 2, h - 6)
            if h == 10 and b + 2 < B:
                norm_rstd(b + 2)
            if 11 <= h < 15 and b + 2 < B:
                norm_apply(b + 2, h - 11)
            if b + 1 < B:
                if h == 5:
                    dist_squares(b + 1)
                if h == 6:
                    dist_sum(b + 1)
                if h == 8:
                    dist_sqrt(b + 1)
                if h == 9 and b + 2 < B:
                    load_geometry(b + 2)

        phase1_end = (got("oproj", B - 1, 1), got("x1st", B - 1, 0), got("x1st", B - 1, 1), got("vo_free"))
        s_w1 = [dsig(f"s_w1_{i}") for i in range(4)]
        s_w2 = [dsig(f"s_w2_{i}") for i in range(4)]
        s_b2 = dsig("s_b2")
        s_w1hi, s_w1lo, s_w2hi, s_w2lo, s_b1m, s_b1 = [sig(n) for n in ("s_w1hi", "s_w1lo", "s_w2hi", "s_w2lo", "s_b1m", "s_b1")]
        s_g = [dsig(f"s_g{i}") for i in range(8)]
        s_gst, s_gag, s_gve, s_grs, s_gap = [sig(n) for n in ("s_gst", "s_gag", "s_gve", "s_grs", "s_gap")]
        s_gtr, s_ghi, s_glo = sig("s_gtr"), sig("s_ghi"), sig("s_glo")
        s_m1, s_gelu, s_hhi, s_hlo, s_m2, s_xb, s_out = [sig(n) for n in ("s_m1", "s_gelu", "s_hhi", "s_hlo", "s_m2", "s_xb", "s_out")]
        s_st2 = [dsig(f"s_st2_{i}") for i in range(8)]
        ps_acc = [ps_s[0], ps_s[1], ps_pt[0], ps_pt[1]]
        ps_m1 = [ps_pv, ps_qk]
        ps_b1 = ps_vo
        out_rows = out.rearrange("b (c p) d -> (b c) p d", p=P)
        for q in (sp, act, dve, pool, pe):
            q.wait(*phase1_end)
        b2_in = sp.do(lambda e: e.dma_start(b_2_sb[:], b_2.to_broadcast([P, D])), s_b2)

        def load_weights(m):
            r = m % 4
            sp.wait(got("w1lo", m - 4), got("b1m", m - 4), got("w2lo", m - 4))
            done["w1in", m] = sp.do(lambda e: e.dma_start(
                w_stage[:, r, :].rearrange("p (k n) -> p k n", k=KT),
                w_1[:, m * P:(m + 1) * P].rearrange("(k p) n -> p k n", p=P)), s_w1[r])
            done["w2in", m] = sp.do(lambda e: e.dma_start(w_stage[:, 4 + r, :], w_2[m * P:(m + 1) * P, :]), s_w2[r])

        def weight_tile(m):
            r = m % 4
            pe.wait(got("w1in", m), got("b1", m - 1))
            for k in range(KT):
                mm = lambda e, k=k: e.matmul(ps_b1[:, m:m + 1], w_stage[:, r, k * P:(k + 1) * P],
                                             cols_sb[:, B_M + k:B_M + k + 1], start=(k == 0), stop=(k == KT - 1))
                done["b1m", m] = pe.do(mm, s_b1m if k == KT - 1 else None)
            act.wait(got("w1in", m), got("w2in", m))
            for k in range(KT):
                hi = w_1_sb[:, HI, k, m * P:(m + 1) * P]
                hid_ = act.do(lambda e, k=k, o=hi: e.activation(o, w_stage[:, r, k * P:(k + 1) * P], ACT.Copy,
                                                                scale=cols_sb[:, G_M + k:G_M + k + 1]), s_w1hi)
                dve.wait(hid_)
                done["w1lo", m] = dve.do(lambda e, k=k, h=hi: e.scalar_tensor_tensor(
                    out=w_1_sb[:, LO, k, m * P:(m + 1) * P], in0=w_stage[:, r, k * P:(k + 1) * P],
                    scalar=cols_sb[:, G_M + k:G_M + k + 1], in1=h.bitcast(F32), op0=ALU.mult, op1=ALU.subtract), s_w1lo)
            w2hi = act.do(lambda e: e.activation(w_2_sb[:, HI, m, :], w_stage[:, 4 + r, :], ACT.Copy), s_w2hi)
            dve.wait(got("b1m", m))
            done["b1", m] = dve.do(lambda e: e.tensor_tensor(bias_1[:, m:m + 1], ps_b1[:, m:m + 1],
                                                             cols_sb[:, B_1 + m:B_1 + m + 1], ALU.add), s_b1)
            pool.wait(w2hi)
            done["w2lo", m] = pool.do(lambda e: e.tensor_tensor(w_2_sb[:, LO, m, :], w_stage[:, 4 + r, :],
                                                                w_2_sb[:, HI, m, :].bitcast(F32), ALU.subtract), s_w2lo)

        def g_load(g):
            for i in range(GT):
                sp.wait(got("gst", g - 2, i), *[got("x1st", 2 * g + 1, tt) for tt in range(2)])
                done["gin", g, i] = sp.do(lambda e, i=i: e.dma_start(x1_g[:, g % 2, i, :], x1_dram[g * GT + i]), s_g[g % 2 * 4 + i])

        def g_stats(g, i):
            dve.wait(got("gin", g, i), got("gap", g - 1, GT - 1))
            st = dve.do(lambda e: e.bn_stats(stats[:, i, :], x1_g[:, g % 2, i, :]), s_gst)
            dve.wait(st)
            done["gag", g] = dve.do(lambda e: e.bn_aggr(mean_var[:, i, :], stats[:, i, :]), s_gag)

        def g_rstd(g):
            dve.wait(got("gag", g))
            ve = dve.do(lambda e: e.tensor_scalar(var_eps[:], mean_var[:, :, 1], LN_EPS, None, ALU.add), s_gve)
            pool.wait(ve)
            done["grs", g] = pool.do(lambda e: e.tensor_tensor(rstd[:], var_eps[:], neg_half[:], ALU.pow), s_grs)

        def g_apply(g, i):
            prev = (g, i - 2) if i >= 2 else (g - 1, i + 2)
            dve.wait(got("grs", g), got("gtr", *prev))
            done["gap", g, i] = dve.do(lambda e: e.tensor_scalar(
                x1_n[:, i % 2, :], x1_g[:, g % 2, i, :], mean_var[:, i, 0:1], rstd[:, i:i + 1], ALU.subtract, ALU.mult), s_gap)
            pool.wait(got("gap", g, i), b2_in)
            done["xb", g, i] = pool.do(lambda e: e.tensor_tensor(x1_g[:, g % 2, i, :], x1_g[:, g % 2, i, :], b_2_sb[:], ALU.add), s_xb)

        def g_transpose(g, i):
            pe.wait(got("gap", g, i), got("glo_last"))
            for k in range(KT):
                tr = lambda e, k=k: e.transpose(ps_tr[:, k * P:(k + 1) * P], x1_n[:, i % 2, k * P:(k + 1) * P], ident[:])
                done["gtr", g, i] = pe.do(tr, s_gtr if k == KT - 1 else None)
            src = ps_tr[:].rearrange("p (k t) -> p k t", k=KT)
            hi, lo = [hT[:, g % 2, part, :, i * P:(i + 1) * P] for part in (HI, LO)]
            act.wait(got("gtr", g, i), got("m1", (g - 2) * MT + MT - 1),
                     *((got("w2lo", MT - 1), got("w1lo", MT - 1), got("b1m", MT - 1)) if g == 1 else ()))
            hi_done = act.do(lambda e: e.activation(hi, src, ACT.Copy), s_ghi)
            dve.wait(hi_done)
            done["glo", g, i] = done["glo_last",] = dve.do(lambda e: e.tensor_tensor(lo, src, hi.bitcast(F32), ALU.subtract), s_glo)

        def mlp_up(s):
            g, m = divmod(s, MT)
            pe.wait(got("glo", g, GT - 1), got("w1lo", m), got("gelu", s - 2))
            for k in range(KT):
                for wp, xp in PASSES:
                    first, last = (k, wp, xp) == (0, 0, 0), (k, wp, xp) == (KT - 1,) + PASSES[-1]
                    mm = lambda e, k=k, wp=wp, xp=xp, f=first, l=last: e.matmul(
                        ps_m1[s % 2][:], w_1_sb[:, wp, k, m * P:(m + 1) * P], hT[:, g % 2, xp, k, :], start=f, stop=l)
                    done["m1", s] = pe.do(mm, s_m1 if last else None)
            act.wait(got("m1", s), got("b1", m), got("hlo", s - 2))
            ge = done["gelu", s] = act.do(lambda e: e.activation(gelu[:, s % 2, :], ps_m1[s % 2][:], ACT.Gelu,
                                                                 bias=bias_1[:, m:m + 1]), s_gelu)
            act.wait(ge, got("m2", s - 3))
            hh = act.do(lambda e: e.activation(hid[:, s % 3, HI, :], gelu[:, s % 2, :], ACT.Copy), s_hhi)
            dve.wait(hh)
            done["hlo", s] = dve.do(lambda e: e.tensor_tensor(hid[:, s % 3, LO, :], gelu[:, s % 2, :],
                                                              hid[:, s % 3, HI, :].bitcast(F32), ALU.subtract), s_hlo)

        def mlp_down(s):
            g, m = divmod(s, MT)
            pe.wait(got("hlo", s), got("w2lo", m))
            for i in range(GT):
                if m == 0:
                    pe.wait(got("out", g - 1, i))
                for hp, wp in PASSES:
                    mm = lambda e, i=i, hp=hp, wp=wp: e.matmul(
                        ps_acc[i][:], hid[:, s % 3, hp, i * P:(i + 1) * P], w_2_sb[:, wp, m, :],
                        start=(m == 0 and (hp, wp) == PASSES[0]), stop=(m == MT - 1 and (hp, wp) == PASSES[-1]))
                    done["m2", s] = pe.do(mm, s_m2 if (hp, wp) == PASSES[-1] else None)
                if m == MT - 1:
                    dve.wait(got("m2", s), got("xb", g, i))
                    done["out", g, i] = dve.do(lambda e, i=i: e.tensor_tensor(
                        x1_g[:, g % 2, i, :], ps_acc[i][:], x1_g[:, g % 2, i, :], ALU.add), s_out)
                    sp.wait(got("out", g, i))
                    done["gst", g, i] = sp.do(lambda e, i=i: e.dma_start(out_rows[g * GT + i], x1_g[:, g % 2, i, :]), s_st2[g % 2 * 4 + i])

        g_load(0)
        for m in range(4):
            load_weights(m)
        for i in range(GT):
            g_stats(0, i)
        g_rstd(0)
        for i in range(GT):
            g_apply(0, i)
            g_transpose(0, i)
        for m in range(2):
            weight_tile(m)
            load_weights(m + 4)
        for s in range(N_GROUPS * MT + 1):
            g, m = divmod(s, MT)
            if s < N_GROUPS * MT:
                mlp_up(s)
            if g == 0:
                for w in (2 * m + 2, 2 * m + 3):
                    if w < MT:
                        weight_tile(w)
                    if w + 4 < MT:
                        load_weights(w + 4)
            if s >= 1:
                mlp_down(s - 1)
            if g + 1 < N_GROUPS:
                if m == 2:
                    g_load(g + 1)
                if 4 <= m < 8:
                    g_stats(g + 1, m - 4)
                if m == 8:
                    g_rstd(g + 1)
                if m in (9, 10):
                    g_apply(g + 1, m - 9)
                if 11 <= m < 15:
                    g_transpose(g + 1, m - 11)
                    if m < 13:
                        g_apply(g + 1, m - 9)
        for i in range(GT):
            for g in (N_GROUPS - 2, N_GROUPS - 1):
                sp.wait(got("gst", g, i))

        block = es.enter_context(nc.Block())
        block.sync(lambda e: sp.run(e))
        block.scalar(lambda e: act.run(e))
        block.vector(lambda e: dve.run(e))
        block.gpsimd(lambda e: pool.run(e))
        block.tensor(lambda e: pe.run(e))


def kernel(**inputs):
    import numpy as np
    import concourse.bacc as bacc
    from concourse.bass_utils import run_bass_kernel_spmd

    a = {k.replace("L0_xattn_", ""): np.asarray(v) for k, v in inputs.items()}
    x = a["x"]
    B, L, D = x.shape

    def columns(v):
        return v.reshape(-1, P).T

    lay = {
        "x": x,
        "ctx": a["ctx_1024"],
        "tok_xy": a["fside_BxS2x2_0"].transpose(0, 2, 1),
        "q_xy": a["fside_BxSx2_0"].reshape(-1, P, 2).transpose(1, 0, 2).reshape(P, -1),
        "mask": a["mask_BxS2_bf1"].view(np.uint8),
        "w_qkv": a["in_proj_w"].T,
        "w_o": a["out_proj_w"].T,
        "w_1": a["mlp_w1"].T,
        "w_2": a["mlp_w2"].T,
        "cols": np.concatenate([columns(a[n]) for n in (
            "q_norm_g", "q_norm_b", "kv_norm_g", "kv_norm_b", "in_proj_b", "mlp_norm_g", "mlp_norm_b", "mlp_b1")], axis=1),
        "b_o": a["out_proj_b"].reshape(1, -1),
        "b_2": a["mlp_b2"].reshape(1, -1),
        "sp_scale": a["spatial_scale"].reshape(1, -1),
        "sp_offset": a["spatial_offset"].reshape(1, -1),
    }
    nc = bacc.Bacc("TRN2", target_bir_lowering=False, num_devices=1)
    arrays, aps = {}, []
    for name, v in lay.items():
        arrays[f"in_{name}"] = np.ascontiguousarray(v)
        aps.append(nc.dram_tensor(f"in_{name}", v.shape, mybir.dt.from_np(v.dtype), kind="ExternalInput").ap())
    out = nc.dram_tensor("out_0", x.shape, F32, kind="ExternalOutput").ap()
    x1 = nc.dram_tensor("x1_scratch", (B * L // P, P, D), F32).ap()
    build_block(nc, *aps, out, x1)
    return run_bass_kernel_spmd(nc, [arrays], core_ids=[0]).results[0]["out_0"]
```

```python
from contextlib import ExitStack

import concourse.bass as bass
from concourse import mybir

F32 = mybir.dt.float32
F32R = mybir.dt.float32r
BF16 = mybir.dt.bfloat16
F16 = mybir.dt.float16
U8 = mybir.dt.uint8
ALU = mybir.AluOpType
ACT = mybir.ActivationFunctionType

P = 128
LN_EPS = 1e-05
P_SCALE = 2.0 ** 14
HI, LO = 0, 1
PASSES = ((HI, HI), (HI, LO), (LO, HI))
PV_PASSES = ((0, 0), (0, 1), (0, 2), (1, 0), (1, 1))


class Signal:

    def __init__(self, sem, step=1):
        self.sem, self.step, self.count = sem, step, 0


class Queue:

    def __init__(self):
        self.ops, self.seen = [], {}

    def wait(self, *marks):
        for mark in marks:
            if mark is None:
                continue
            signal, value = mark
            if self.seen.get(id(signal), 0) < value:
                self.seen[id(signal)] = value
                self.ops.append(lambda e, s=signal.sem, v=value: e.wait_ge(s, v))

    def do(self, make, signal=None):
        if signal is None:
            self.ops.append(make)
            return None
        signal.count += signal.step
        self.ops.append(lambda e, s=signal: make(e).then_inc(s.sem, s.step))
        return signal, signal.count

    def run(self, engine):
        for op in self.ops:
            op(engine)


def build_block(nc, x, ctx, tok_xy, q_xy, mask, w_qkv, w_o, w_1, w_2, cols, b_o, b_2, sp_scale, sp_offset, out, x1_dram):
    B, L, D = x.shape
    T = ctx.shape[1]
    H = sp_scale.shape[1]
    HD = D // H
    FF = w_1.shape[1]
    KT = D // P
    LC, TC = L // P, T // P
    HG, HPG = H // 4, 4
    MT = FF // P
    N_ITEMS = B * H
    GROUP_TOK = 512
    N_GROUPS = B * L // GROUP_TOK
    GT = GROUP_TOK // P
    SCORE_SCALE = float(HD) ** -0.5
    assert (L, T, D, HD, KT, HG) == (256, 256, 512, 32, 4, 4)

    es = ExitStack()
    with es:
        ARENA = 16512
        top = [ARENA]

        def sb(name, shape, dt, at=None):
            size = mybir.dt.size(dt)
            for s in shape[1:]:
                size *= s
            off = top[0] if at is None else at
            if at is None:
                top[0] += (size + 31) // 32 * 32
                assert top[0] <= 229344, (name, top[0])
            return nc.alloc_sbuf_tensor_at(name, shape, dt, offset=off)

        ident = sb("ident", [P, P], F32)
        cols_sb = sb("cols", [P, cols.shape[1]], F32)
        scale_neg = sb("scale_neg", [P, H], F32)
        offset_sb = sb("offset", [P, H], F32)
        q_neg = sb("q_neg", [P, B * LC * 2], F32)
        gq = sb("gq", [P, KT], F32)
        bias_qkv = sb("bias_qkv", [P, 12], F32)
        bias_1 = sb("bias_1", [P, MT], F32)
        neg_half = sb("neg_half", [P, 4], F32)
        stats = sb("stats", [P, 4, 6], F32)
        mean_var = sb("mean_var", [P, 4, 2], F32)
        var_eps = sb("var_eps", [P, 4], F32)
        rstd = sb("rstd", [P, 4], F32)
        phase1 = top[0]
        SOFT_RING = 7
        row_stats = sb("row_stats", [P, 3, SOFT_RING, LC], F32)
        neg_max, row_sum, row_inv = [row_stats[:, i, :, :] for i in range(3)]
        w_qkv_sb = sb("w_qkv_sb", [P, 2, KT, 3 * D], F32R)
        w_o_sb = sb("w_o_sb", [P, 2, KT, D], F32R)
        xT = sb("xT", [P, 2, 2, 2, KT, L], F32R)
        STACK_RING = 3
        stack = sb("stack", [P, STACK_RING, HPG, 2, L], F32R)
        qk_parts = sb("qk_parts", [P, 3, 2, L], F32R)
        v_parts = sb("v_parts", [P, 2, TC, 3, D], BF16)
        v_rest = sb("v_rest", [P, D], F32)
        attnT = sb("attnT", [P, 2, 2, HG, L], F32R)
        attn_y = sb("attn_y", [P, L], F32)
        raw = sb("raw", [P, 4, D], F32)
        x1_t = sb("x1_t", [P, 2, D], F32)
        dist = sb("dist", [P, 2, LC, T], F32)
        tok_rows = sb("tok_rows", [P, 2, T], F32)
        sq = sb("sq", [P, LC, T], F32)
        mask_u8 = sb("mask_u8", [P, T], U8)
        mask_row = sb("mask_row", [P, 2, T], F32)
        soft = sb("soft", [P, SOFT_RING, LC, T], F32)
        PT_RING = 6
        pT = sb("pT", [P, PT_RING, 2, TC * L], F16)

        top[0] = phase1
        w_1_sb = sb("w_1_sb", [P, 2, KT, FF], F32R)
        w_2_sb = sb("w_2_sb", [P, 2, MT, D], F32R)
        hT = sb("hT", [P, 2, 2, KT, GROUP_TOK], F32R)
        hid = sb("hid", [P, 3, 2, GROUP_TOK], F32R)
        gelu = sb("gelu", [P, 2, GROUP_TOK], F32)
        x1_g = sb("x1_g", [P, 2, GT, D], F32)
        x1_n = sb("x1_n", [P, 2, D], F32)
        b_o_sb = sb("b_o", [P, D], F32)
        b_2_sb = sb("b_2", [P, D], F32)
        w_stage = sb("w_stage", [P, 8, D], F32, at=phase1 + (2 * KT * FF + 2 * MT * D + 2 * KT * GROUP_TOK) * 4)

        def bank(name):
            return es.enter_context(nc.psum_tensor(name, [P, 512], F32))

        ps_s = [bank("ps_s0"), bank("ps_s1")]
        ps_pt = [bank("ps_pt0"), bank("ps_pt1")]
        ps_pv = bank("ps_pv")
        ps_tr = bank("ps_tr")
        ps_qk = bank("ps_qk")
        ps_vo = bank("ps_vo")

        def sig(name, step=1):
            return Signal(es.enter_context(nc.semaphore(name)), step)

        def dsig(name):
            return sig(name, 16)

        pe, act, dve, pool, sp = Queue(), Queue(), Queue(), Queue(), Queue()

        s_cols, s_small, s_bo = dsig("s_cols"), dsig("s_small"), dsig("s_bo")
        cols_in = sp.do(lambda e: e.dma_start(cols_sb[:], cols), s_cols)
        small_in = None
        for dst, src in ((scale_neg[:], sp_scale.to_broadcast([P, H])), (offset_sb[:], sp_offset.to_broadcast([P, H])),
                         (q_neg[:], q_xy)):
            small_in = sp.do(lambda e, d=dst, s=src: e.dma_start(d, s), s_small)
        G_Q, B_Q, G_KV, B_KV, B_IN, G_M, B_M, B_1 = 0, 4, 8, 12, 16, 28, 32, 36

        s_id, s_cst = sig("s_id"), sig("s_cst")
        pool.wait(pool.do(lambda e: e.memset(ident[:], 0.0), s_id))
        ident_done = pool.do(lambda e: e.affine_select(out=ident[:], in_=ident[:], compare_op=ALU.not_equal, fill=1.0,
                                                       base=0, pattern=[[-1, P]], channel_multiplier=1), s_id)
        pool.wait(ident_done)
        ones_done = pool.do(lambda e: e.memset(stack[96:97, :, :, 0, :].bitcast(F32), 1.0), s_id)
        pool.wait(ones_done)
        half_done = pool.do(lambda e: e.memset(neg_half[:], -0.5), s_id)
        dve.wait(cols_in, small_in)
        dve.do(lambda e: e.tensor_scalar(scale_neg[:], scale_neg[:], -1.0, None, ALU.mult), s_cst)
        gq_done = dve.do(lambda e: e.tensor_scalar(gq[:], cols_sb[:, G_Q:G_Q + KT], SCORE_SCALE, None, ALU.mult), s_cst)
        consts_done = dve.do(lambda e: e.tensor_scalar(q_neg[:], q_neg[:], -1.0, None, ALU.mult), s_cst)

        s_w = [dsig("s_w0"), dsig("s_w1")]
        s_w_hi, s_w_lo, s_bmm, s_bcol = sig("s_w_hi"), sig("s_w_lo"), sig("s_bmm"), sig("s_bcol")
        stages = (raw[:], soft[:, 0:4, :, :].rearrange("p a b c -> p a (b c)"))
        w_lo_done = {}
        bmm_done = None

        def weight_parts(sec, k):
            if sec < 3:
                return [w_qkv_sb[:, part, k, sec * D:(sec + 1) * D] for part in (HI, LO)]
            return [w_o_sb[:, part, k, :] for part in (HI, LO)]

        for sec in range(4):
            stage = stages[sec % 2]
            src = w_o if sec == 3 else w_qkv[:, sec * D:(sec + 1) * D]
            sp.wait(w_lo_done.get(sec - 2), bmm_done if sec >= 2 else None)
            w_in = sp.do(lambda e, d=stage, s=src.rearrange("(k p) n -> p k n", p=P): e.dma_start(d, s), s_w[sec % 2])
            if sec < 3:
                b_ln = B_Q if sec == 0 else B_KV
                pe.wait(w_in, cols_in)
                for m in range(KT):
                    for k in range(KT):
                        mm = lambda e, m=m, k=k, sec=sec, st=stage, b=b_ln: e.matmul(
                            ps_tr[:, sec * KT + m:sec * KT + m + 1], st[:, k, m * P:(m + 1) * P],
                            cols_sb[:, b + k:b + k + 1], start=(k == 0), stop=(k == KT - 1))
                        last = pe.do(mm, s_bmm if (m, k) == (KT - 1, KT - 1) else None)
                bmm_done = last
            act.wait(w_in, gq_done)
            dve.wait(w_in)
            for k in range(KT):
                hi, lo = weight_parts(sec, k)
                g = {0: gq[:, k:k + 1], 3: 1.0}.get(sec, cols_sb[:, G_KV + k:G_KV + k + 1])
                hi_done = act.do(lambda e, o=hi, i=stage[:, k, :], g=g: e.activation(o, i, ACT.Copy, scale=g), s_w_hi)
                dve.wait(hi_done, gq_done)
                w_lo_done[sec] = dve.do(lambda e, o=lo, i=stage[:, k, :], g=g, h=hi: e.scalar_tensor_tensor(
                    out=o, in0=i, scalar=g, in1=h.bitcast(F32), op0=ALU.mult, op1=ALU.subtract), s_w_lo)
        stage_free = (w_lo_done[3], w_lo_done[2], bmm_done)
        dve.wait(bmm_done)
        dve.wait(dve.do(lambda e: e.tensor_tensor(bias_qkv[:], ps_tr[:, 0:12], cols_sb[:, B_IN:B_IN + 12], ALU.add), s_bcol))
        bcol_done = dve.do(lambda e: e.tensor_scalar(bias_qkv[:, 0:KT], bias_qkv[:, 0:KT], SCORE_SCALE, None, ALU.mult), s_bcol)

        s_raw = [dsig(f"s_raw{i}") for i in range(4)]
        s_st, s_ag, s_ve, s_rs, s_ap = sig("s_st"), sig("s_ag"), sig("s_ve"), sig("s_rs"), sig("s_ap")
        s_xtr, s_xhi, s_xlo = sig("s_xtr"), sig("s_xhi"), sig("s_xlo")
        s_qk, s_qkhi, s_qklo = sig("s_qk"), sig("s_qkhi"), sig("s_qklo")
        s_stack = [dsig(f"s_stack{i}") for i in range(4)]
        s_v, s_va, s_vr, s_vb, s_vc = [sig(n) for n in ("s_v", "s_va", "s_vr", "s_vb", "s_vc")]
        s_xy, s_sq, s_d2, s_dist = dsig("s_xy"), sig("s_sq"), sig("s_d2"), sig("s_dist")
        s_mu, s_mrow = dsig("s_mu"), sig("s_mrow")
        s_bias, s_score, s_max, s_exp, s_inv, s_norm = [sig(n) for n in ("s_bias", "s_score", "s_max", "s_exp", "s_inv", "s_norm")]
        s_t, s_pthi, s_ptlo, s_pv, s_y, s_ahi, s_alo = [sig(n) for n in ("s_t", "s_pthi", "s_ptlo", "s_pv", "s_y", "s_ahi", "s_alo")]
        s_o, s_res, s_x1 = sig("s_o"), [dsig("s_res0"), dsig("s_res1")], sig("s_x1")
        s_x1st = [dsig("s_x1st0"), dsig("s_x1st1")]
        done = {}
        FIRST_USE = ("xlo_last", "qklo_last", "vo_free", "vc_last", "glo_last")

        def got(*key):
            if key not in done and (key[0] in FIRST_USE or any(i < 0 for i in key[1:])):
                return None
            return done[key]

        x_rows = x.rearrange("b (c p) d -> (b c) p d", p=P)
        c_rows = ctx.rearrange("b (c p) d -> (b c) p d", p=P)

        def load_tile(b, i):
            src = (x_rows if i < 2 else c_rows)[b * 2 + i % 2]
            sp.wait(got("xtr", b - 1, i), *(stage_free if b == 0 else ()))
            done["raw", b, i] = sp.do(lambda e: e.dma_start(raw[:, i, :], src), s_raw[i])

        def load_geometry(b):
            sp.wait(got("sq", b - 1))
            done["xy", b] = sp.do(lambda e, b=b: e.dma_start(
                tok_rows[:], tok_xy[b:b + 1].to_broadcast([P, 2, T])), s_xy)
            sp.wait(got("mrow_conv", b - 1))
            done["mask", b] = sp.do(lambda e, b=b: e.dma_start(mask_u8[96:97, :], mask[b:b + 1, :]), s_mu)

        def norm_stats(b, i):
            dve.wait(got("raw", b, i), got("ap", b - 1, i), got("rstd", b - 1, i // 2))
            st = dve.do(lambda e: e.bn_stats(stats[:, i, :], raw[:, i, :]), s_st)
            dve.wait(st)
            done["ag", b, i] = dve.do(lambda e: e.bn_aggr(mean_var[:, i, :], stats[:, i, :]), s_ag)

        def norm_eps(b, which):
            pair = slice(2 * which, 2 * which + 2)
            dve.wait(got("ag", b, 2 * which + 1), got("rstd", b - 1, which))
            done["ve", b, which] = dve.do(lambda e: e.tensor_scalar(
                var_eps[:, pair], mean_var[:, pair, 1], LN_EPS, None, ALU.add), s_ve)

        def norm_rstd(b, which):
            pair = slice(2 * which, 2 * which + 2)
            pool.wait(got("ve", b, which), half_done, got("ap", b - 1, 2 * which + 1))
            done["rstd", b, which] = pool.do(lambda e: e.tensor_tensor(rstd[:, pair], var_eps[:, pair], neg_half[:, pair], ALU.pow), s_rs)

        def norm_apply(b, i):
            dve.wait(got("rstd", b, i // 2))
            done["ap", b, i] = dve.do(lambda e: e.tensor_scalar(
                raw[:, i, :], raw[:, i, :], mean_var[:, i, 0:1], rstd[:, i:i + 1], ALU.subtract, ALU.mult), s_ap)

        def x_transpose(b, i):
            pe.wait(got("ap", b, i), got("xlo_last"), ident_done, bcol_done)
            for k in range(KT):
                tr = lambda e, i=i, k=k: e.transpose(ps_tr[:, k * P:(k + 1) * P], raw[:, i, k * P:(k + 1) * P], ident[:])
                last = pe.do(tr, s_xtr if k == KT - 1 else None)
            done["xtr", b, i] = last

        def x_parts(b, i):
            ring, which, tok = b % 2, i // 2, (i % 2) * P
            src = ps_tr[:].rearrange("p (k t) -> p k t", k=KT)
            hi = xT[:, ring, which, HI, :, tok:tok + P]
            lo = xT[:, ring, which, LO, :, tok:tok + P]
            act.wait(got("xtr", b, i), got("qk", 4 * (b - 2) + 3, 1), got("vproj", b - 2, 1))
            hi_done = act.do(lambda e, o=hi, s=src: e.activation(o, s, ACT.Copy), s_xhi)
            dve.wait(hi_done)
            done["xlo", b, i] = done["xlo_last",] = dve.do(lambda e, o=lo, s=src, h=hi: e.tensor_tensor(
                o, s, h.bitcast(F32), ALU.subtract), s_xlo)

        def qk_steps(G, which):
            b, hg = divmod(G, HG)
            ring = b % 2
            steps = []
            for k in range(KT):
                for wp, xp in PASSES:
                    first, last = (k, wp, xp) == (0, 0, 0), (k, wp, xp) == (KT - 1,) + PASSES[-1]
                    col = which * D + hg * P
                    mm = lambda e, k=k, wp=wp, xp=xp, f=first, l=last, c=col: e.matmul(
                        ps_qk[:, which * L:(which + 1) * L], w_qkv_sb[:, wp, k, c:c + P], xT[:, ring, which, xp, k, :], start=f, stop=l)

                    def step(mm=mm, f=first, l=last):
                        if f:
                            pe.wait(got("xlo", b, 2 * which + 1), got("qklo_last"), w_lo_done[1])
                        r = pe.do(mm, s_qk if l else None)
                        if l:
                            done["qk", G, which] = r
                    steps.append(step)
            return steps

        def qk_split(G):
            src, col, hi_of, lo_of = [], [], [], []
            for which in range(2):
                src.append(ps_qk[:, which * L:(which + 1) * L])
                col.append(bias_qkv[:, which * KT + G % HG:which * KT + G % HG + 1])
                his = slice(0, 2) if which else slice(1, 3)
                hi_of.append(qk_parts[:, his, which, :])
                lo_of.append(qk_parts[:, 2 if which else 0, which, :])
            act.wait(got("qk", G, 1), got("stack", G - 1), bcol_done)
            for which in range(2):
                twice = src[which].rearrange("p (o l) -> p o l", o=1).to_broadcast([P, 2, L])
                hi_done = act.do(lambda e, o=hi_of[which], i=twice, c=col[which]: e.activation(o, i, ACT.Identity, bias=c), s_qkhi)
            dve.wait(hi_done)
            for which in range(2):
                done["qklo", G] = done["qklo_last",] = dve.do(
                    lambda e, o=lo_of[which], i=src[which], h=qk_parts[:, 1, which, :], c=col[which]: e.scalar_tensor_tensor(
                        out=o, in0=i, scalar=c, in1=h.bitcast(F32), op0=ALU.add, op1=ALU.subtract), s_qklo)

        def stack_copies(G):
            b, ring = G // HG, G % STACK_RING
            sp.wait(got("qklo", G), got("score", 4 * (G - STACK_RING) + 3), got("mrow", b), ones_done)
            for j in range(HPG):
                src = qk_parts[32 * j:32 * j + 32, :, :, :].bitcast(F32).rearrange("p r w l -> p r (w l)")
                dst = stack[0:96, ring, j, :, :].bitcast(F32).rearrange("p w l -> p (w l)")
                sp.do(lambda e, d=dst, s=src: e.dma_start(d, s), s_stack[ring])
            dst = stack[96:97, ring, :, 1, :].bitcast(F32)
            src = mask_row[96:97, b % 2, :].rearrange("p (o t) -> p o t", o=1).to_broadcast([1, HPG, T])
            done["stack", G] = sp.do(lambda e: e.dma_start(dst, src), s_stack[ring])

        def mask_steps(b):
            row, src = mask_row[96:97, b % 2, :], mask_u8[96:97, :]
            dve.wait(got("mask", b), got("stack", 4 * (b - 1) - 1))
            m1 = dve.do(lambda e: e.tensor_scalar(row, src, 0.0, -3.0e38, ALU.is_equal, ALU.mult), s_mrow)
            done["mrow_conv", b] = m1
            dve.wait(m1)
            done["mrow", b] = dve.do(lambda e: e.tensor_scalar(row, row, 3.0e38, None, ALU.mult), s_mrow)

        def v_steps(b, tt):
            ring = b % 2
            steps = []
            for k in range(KT):
                for xp, wp in PASSES:
                    first, last = (k, xp, wp) == (0, 0, 0), (k, xp, wp) == (KT - 1,) + PASSES[-1]
                    mm = lambda e, k=k, wp=wp, xp=xp, f=first, l=last: e.matmul(
                        ps_vo[:], xT[:, ring, 1, xp, k, tt * P:(tt + 1) * P], w_qkv_sb[:, wp, k, 2 * D:3 * D], start=f, stop=l)

                    def step(mm=mm, f=first, l=last):
                        if f:
                            pe.wait(got("xlo", b, 3), got("vo_free"), w_lo_done[2])
                        r = pe.do(mm, s_v if l else None)
                        if l:
                            done["vproj", b, tt] = r
                    steps.append(step)
            return steps

        def v_split(b, tt):
            first = v_parts[:, b % 2, tt, 0, :]
            act.wait(got("vproj", b, tt), got("pv", 4 * (b - 2) + 3))
            va = act.do(lambda e: e.activation(first, ps_vo[:], ACT.Copy), s_va)
            dve.wait(va, got("vc_last"))
            done["vr", b, tt] = done["vo_free",] = dve.do(lambda e: e.tensor_tensor(v_rest[:], ps_vo[:], first, ALU.subtract), s_vr)

        def v_second(b, tt):
            act.wait(got("vr", b, tt))
            done["vb", b, tt] = act.do(lambda e: e.activation(v_parts[:, b % 2, tt, 1, :], v_rest[:], ACT.Copy), s_vb)

        def v_third(b, tt):
            pool.wait(got("vb", b, tt))
            done["v", b, tt] = done["vc_last",] = pool.do(lambda e: e.tensor_tensor(
                v_parts[:, b % 2, tt, 2, :], v_rest[:], v_parts[:, b % 2, tt, 1, :], ALU.subtract), s_vc)

        def dist_square(b, c):
            act.wait(got("xy", b), consts_done, got("d2", b - 1), got("bias", H * (b - 1) - 1))
            for lc in range(LC):
                dst = (dist[:, b % 2, lc, :], sq[:, lc, :])[c]
                col = (b * LC + lc) * 2 + c
                done["sq", b] = act.do(lambda e, o=dst, q=col: e.activation(o, tok_rows[:, c, :], ACT.Square, bias=q_neg[:, q:q + 1]), s_sq)

        def dist_sum(b):
            dve.wait(got("sq", b))
            d = dist[:, b % 2, :, :]
            done["d2", b] = dve.do(lambda e: e.tensor_tensor(d, d, sq[:], ALU.add), s_d2)

        def dist_floor(b):
            dve.wait(got("d2", b))
            d = dist[:, b % 2, :, :]
            done["d2max", b] = dve.do(lambda e: e.tensor_scalar(d, d, 0.0, None, ALU.max), s_d2)

        def dist_sqrt(b):
            d = dist[:, b % 2, :, :]
            act.wait(got("d2max", b))
            done["dist", b] = act.do(lambda e: e.activation(d, d, ACT.Sqrt), s_dist)

        def bias_tile(i):
            b, h = divmod(i, H)
            pool.wait(got("dist", b), got("t", i - SOFT_RING), consts_done, *(stage_free if i < SOFT_RING else ()))
            done["bias", i] = pool.do(lambda e: e.tensor_scalar(
                soft[:, i % SOFT_RING, :, :], dist[:, b % 2, :, :], scale_neg[:, h:h + 1], offset_sb[:, h:h + 1], ALU.mult, ALU.add), s_bias)

        def scores(i):
            b, h = divmod(i, H)
            ring, j = (i // 4) % STACK_RING, i % 4
            pe.wait(got("stack", i // 4), got("max", i - 2))
            for lc in range(LC):
                mm = lambda e, lc=lc: e.matmul(ps_s[i % 2][:, lc * T:(lc + 1) * T], stack[0:97, ring, j, 0, lc * P:(lc + 1) * P],
                                               stack[0:97, ring, j, 1, :], start=True, stop=True)
                r = pe.do(mm, s_score if lc == LC - 1 else None)
            done["score", i] = r

        def score_max(i):
            dve.wait(got("score", i), got("bias", i), got("exp", i - SOFT_RING))
            for lc in range(LC):
                done["max", i] = done["max", i, lc] = dve.do(lambda e, lc=lc: e.tensor_tensor_reduce(
                    soft[:, i % SOFT_RING, lc, :], ps_s[i % 2][:, lc * T:(lc + 1) * T], soft[:, i % SOFT_RING, lc, :], -1.0, 3.0e38,
                    ALU.add, ALU.min, neg_max[:, i % SOFT_RING, lc:lc + 1]), s_max)

        def exps(i):
            act.wait(got("inv", i - SOFT_RING))
            for lc in range(LC):
                act.wait(got("max", i, lc))
                done["exp", i] = act.do(lambda e, lc=lc: e.activation(
                    soft[:, i % SOFT_RING, lc, :], soft[:, i % SOFT_RING, lc, :], ACT.Exp, scale=-1.0, bias=neg_max[:, i % SOFT_RING, lc:lc + 1],
                    accum_out=row_sum[:, i % SOFT_RING, lc:lc + 1]), s_exp)

        def inverse(i):
            dve.wait(got("exp", i), got("norm", i - SOFT_RING))
            done["inv", i] = dve.do(lambda e: e.reciprocal(row_inv[:, i % SOFT_RING, :], row_sum[:, i % SOFT_RING, :]), s_inv)

        def normalise(i):
            pool.wait(got("inv", i))
            for lc in range(LC):
                done["norm", i] = pool.do(lambda e, lc=lc: e.tensor_scalar(
                    soft[:, i % SOFT_RING, lc, :], soft[:, i % SOFT_RING, lc, :], row_inv[:, i % SOFT_RING, lc:lc + 1], P_SCALE, ALU.mult, ALU.mult), s_norm)

        def p_transpose(i):
            pe.wait(got("norm", i), got("ptlo", i - 2))
            for tc in range(TC):
                for lc in range(LC):
                    tr = lambda e, tc=tc, lc=lc: e.transpose(
                        ps_pt[i % 2][:, tc * L + lc * P:tc * L + (lc + 1) * P], soft[:, i % SOFT_RING, lc, tc * P:(tc + 1) * P], ident[:])
                    r = pe.do(tr, s_t if (tc, lc) == (TC - 1, LC - 1) else None)
            done["t", i] = r

        def p_parts(i):
            hi, lo = pT[:, i % PT_RING, 0, :], pT[:, i % PT_RING, 1, :]
            act.wait(got("t", i), got("pv", (i - PT_RING) // 4) if i >= PT_RING else None)
            hi_done = act.do(lambda e: e.activation(hi, ps_pt[i % 2][:], ACT.Copy), s_pthi)
            dve.wait(hi_done)
            done["ptlo", i] = dve.do(lambda e: e.tensor_tensor(lo, ps_pt[i % 2][:], hi, ALU.subtract), s_ptlo)

        ROUNDS = [(tc, pp, vp) for tc in range(TC) for pp, vp in PV_PASSES]

        def attend(G):
            b, hg = divmod(G, HG)
            pe.wait(got("ptlo", 4 * G + 3), got("v", b, 1), got("y", G - 1))
            for n, (tc, pp, vp) in enumerate(ROUNDS):
                for j in range(HPG):
                    h = hg * HPG + j
                    mm = lambda e, tc=tc, pp=pp, vp=vp, j=j, h=h, n=n: e.matmul(
                        ps_pv[32 * j:32 * j + 32, 0:L], v_parts[:, b % 2, tc, vp, h * HD:(h + 1) * HD],
                        pT[:, (4 * G + j) % PT_RING, pp, tc * L:(tc + 1) * L], start=(n == 0), stop=(n == len(ROUNDS) - 1))
                    r = pe.do(mm, s_pv if (n, j) == (len(ROUNDS) - 1, HPG - 1) else None)
            done["pv", G] = r

        def attn_scale(G):
            hg = G % HG
            dve.wait(got("pv", G), got("alo", G - 1), bcol_done)
            done["y", G] = dve.do(lambda e: e.tensor_scalar(
                attn_y[:], ps_pv[:, 0:L], 1.0 / P_SCALE, bias_qkv[:, 2 * KT + hg:2 * KT + hg + 1], ALU.mult, ALU.add), s_y)

        def attn_hi(G):
            b, hg = divmod(G, HG)
            act.wait(got("y", G), got("oproj", b - 2, 1))
            done["ahi", G] = act.do(lambda e: e.activation(attnT[:, b % 2, HI, hg, :], attn_y[:], ACT.Copy), s_ahi)

        def attn_lo(G):
            b, hg = divmod(G, HG)
            pool.wait(got("ahi", G))
            done["alo", G] = pool.do(lambda e: e.tensor_tensor(
                attnT[:, b % 2, LO, hg, :], attn_y[:], attnT[:, b % 2, HI, hg, :].bitcast(F32), ALU.subtract), s_alo)

        def o_steps(b, tt):
            steps = []
            for k in range(KT):
                for ap_, wp in PASSES:
                    first, last = (k, ap_, wp) == (0, 0, 0), (k, ap_, wp) == (KT - 1,) + PASSES[-1]
                    mm = lambda e, k=k, wp=wp, ap_=ap_, f=first, l=last: e.matmul(
                        ps_vo[:], attnT[:, b % 2, ap_, k, tt * P:(tt + 1) * P], w_o_sb[:, wp, k, :], start=f, stop=l)

                    def step(mm=mm, f=first, l=last):
                        if f:
                            pe.wait(got("alo", 4 * b + 3), got("vo_free"), w_lo_done[3])
                        r = pe.do(mm, s_o if l else None)
                        if l:
                            done["oproj", b, tt] = r
                    steps.append(step)
            return steps

        def load_residual(b):
            for tt in range(LC):
                sp.wait(got("x1st", b - 1, tt))
                done["res", b, tt] = sp.do(lambda e, tt=tt: e.dma_start(x1_t[:, tt, :], x_rows[b * 2 + tt]), s_res[tt])

        def add_residual(b, tt):
            dve.wait(got("oproj", b, tt), got("res", b, tt))
            r = done["vo_free",] = dve.do(lambda e: e.tensor_tensor(x1_t[:, tt, :], ps_vo[:], x1_t[:, tt, :], ALU.add), s_x1)
            sp.wait(r)
            done["x1st", b, tt] = sp.do(lambda e: e.dma_start(x1_dram[b * 2 + tt], x1_t[:, tt, :]), s_x1st[tt])

        fill_vo, fill_qk = [], []
        ITEM, GROUP, BATCH = 1, HPG, H
        CTX, X = 1, 0

        def fill(queue, n):
            for step in queue[:n]:
                step()
            del queue[:n]

        TILES = (2, 3, 0, 1)

        def tiles(first, step):
            return [(BATCH, first + 4 * n, lambda b, i=i: step(b, i)) for n, i in enumerate(TILES)]

        def halves(first, step, apart=4):
            return [(BATCH, first + apart * n, lambda b, n=n: step(b, n)) for n in range(2)]

        schedule = [
            (ITEM, -1, scores),
            (ITEM, 0, score_max),
            (ITEM, 2, inverse),
            (ITEM, 5, p_parts),
            (GROUP, -7, qk_split),
            (GROUP, -7, stack_copies),
            *halves(-10, v_split),
            *halves(30, add_residual),
            *tiles(-25, x_parts),
            (GROUP, 11, attn_scale),
            (ITEM, 1, exps),
            *halves(-9, v_second),
            (GROUP, 12, attn_hi),
            *tiles(-36, norm_stats),
            (BATCH, -31, lambda b: norm_eps(b, CTX)),
            (BATCH, -30, lambda b: norm_rstd(b, CTX)),
            (BATCH, -23, lambda b: norm_eps(b, X)),
            (BATCH, -22, lambda b: norm_rstd(b, X)),
            *tiles(-28, norm_apply),
            *halves(-12, dist_square),
            (BATCH, -10, mask_steps),
            (BATCH, -6, dist_sum),
            (BATCH, -4, dist_floor),
            (BATCH, -2, dist_sqrt),
            (ITEM, 3, normalise),
            (ITEM, -1, bias_tile),
            *halves(-8, v_third),
            (GROUP, 12, attn_lo),
            (ITEM, 4, p_transpose),
            (GROUP, 9, attend),
            (GROUP, -10, lambda G: fill_qk.extend(qk_steps(G, 0) + qk_steps(G, 1))),
            *halves(-13, lambda b, tt: fill_vo.extend(v_steps(b, tt))),
            *halves(27, lambda b, tt: fill_vo.extend(o_steps(b, tt))),
            *tiles(-26, x_transpose),
            *tiles(-41, load_tile),
            (BATCH, -17, load_geometry),
            (BATCH, 20, load_residual),
        ]
        QK_FILL, VO_FILL = (6, 0, 12, 6), (5, 2, 0, 5)
        for slot in range(min(first for _, first, _ in schedule), N_ITEMS - H + 35):
            for every, first, step in schedule:
                k, rest = divmod(slot - first, every)
                if rest == 0 and 0 <= k < N_ITEMS // every:
                    step(k)
            fill(fill_qk, QK_FILL[slot % HPG])
            fill(fill_vo, VO_FILL[slot % HPG])

        phase1_end = (got("oproj", B - 1, 1), got("x1st", B - 1, 0), got("x1st", B - 1, 1), got("vo_free"))
        s_w1 = [dsig(f"s_w1_{i}") for i in range(4)]
        s_w2 = [dsig(f"s_w2_{i}") for i in range(4)]
        s_b2 = dsig("s_b2")
        s_w1hi, s_w1lo, s_w2hi, s_w2lo, s_b1m, s_b1 = [sig(n) for n in ("s_w1hi", "s_w1lo", "s_w2hi", "s_w2lo", "s_b1m", "s_b1")]
        s_g = [dsig(f"s_g{i}") for i in range(8)]
        s_gst, s_gag, s_gve, s_grs, s_gap = [sig(n) for n in ("s_gst", "s_gag", "s_gve", "s_grs", "s_gap")]
        s_gbo = sig("s_gbo")
        s_gtr, s_ghi, s_glo = sig("s_gtr"), sig("s_ghi"), sig("s_glo")
        s_m1, s_gelu, s_hhi, s_hlo, s_m2, s_xb, s_out = [sig(n) for n in ("s_m1", "s_gelu", "s_hhi", "s_hlo", "s_m2", "s_xb", "s_out")]
        s_st2 = [dsig(f"s_st2_{i}") for i in range(8)]
        ps_acc = [ps_s[0], ps_s[1], ps_pt[0], ps_pt[1]]
        ps_m1 = [ps_pv, ps_qk]
        ps_b1 = ps_vo
        out_rows = out.rearrange("b (c p) d -> (b c) p d", p=P)
        for q in (sp, act, dve, pool, pe):
            q.wait(*phase1_end)
        bo_in = sp.do(lambda e: e.dma_start(b_o_sb[:], b_o.to_broadcast([P, D])), s_bo)
        b2_in = sp.do(lambda e: e.dma_start(b_2_sb[:], b_2.to_broadcast([P, D])), s_b2)

        def load_weights(m):
            r = m % 4
            sp.wait(got("w1lo", m - 4), got("b1m", m - 4), got("w2lo", m - 4))
            done["w1in", m] = sp.do(lambda e: e.dma_start(
                w_stage[:, r, :].rearrange("p (k n) -> p k n", k=KT),
                w_1[:, m * P:(m + 1) * P].rearrange("(k p) n -> p k n", p=P)), s_w1[r])
            done["w2in", m] = sp.do(lambda e: e.dma_start(w_stage[:, 4 + r, :], w_2[m * P:(m + 1) * P, :]), s_w2[r])

        def weight_tile(m):
            r = m % 4
            pe.wait(got("w1in", m), got("b1", m - 1))
            for k in range(KT):
                mm = lambda e, k=k: e.matmul(ps_b1[:, m:m + 1], w_stage[:, r, k * P:(k + 1) * P],
                                             cols_sb[:, B_M + k:B_M + k + 1], start=(k == 0), stop=(k == KT - 1))
                done["b1m", m] = pe.do(mm, s_b1m if k == KT - 1 else None)
            act.wait(got("w1in", m), got("w2in", m))
            for k in range(KT):
                hi = w_1_sb[:, HI, k, m * P:(m + 1) * P]
                hid_ = act.do(lambda e, k=k, o=hi: e.activation(o, w_stage[:, r, k * P:(k + 1) * P], ACT.Copy,
                                                                scale=cols_sb[:, G_M + k:G_M + k + 1]), s_w1hi)
                dve.wait(hid_)
                done["w1lo", m] = dve.do(lambda e, k=k, h=hi: e.scalar_tensor_tensor(
                    out=w_1_sb[:, LO, k, m * P:(m + 1) * P], in0=w_stage[:, r, k * P:(k + 1) * P],
                    scalar=cols_sb[:, G_M + k:G_M + k + 1], in1=h.bitcast(F32), op0=ALU.mult, op1=ALU.subtract), s_w1lo)
            w2hi = act.do(lambda e: e.activation(w_2_sb[:, HI, m, :], w_stage[:, 4 + r, :], ACT.Copy), s_w2hi)
            dve.wait(got("b1m", m))
            done["b1", m] = dve.do(lambda e: e.tensor_tensor(bias_1[:, m:m + 1], ps_b1[:, m:m + 1],
                                                             cols_sb[:, B_1 + m:B_1 + m + 1], ALU.add), s_b1)
            pool.wait(w2hi)
            done["w2lo", m] = pool.do(lambda e: e.tensor_tensor(w_2_sb[:, LO, m, :], w_stage[:, 4 + r, :],
                                                                w_2_sb[:, HI, m, :].bitcast(F32), ALU.subtract), s_w2lo)

        def g_load(g):
            for i in range(GT):
                sp.wait(got("gst", g - 2, i), *[got("x1st", 2 * g + 1, tt) for tt in range(2)])
                done["gin", g, i] = sp.do(lambda e, i=i: e.dma_start(x1_g[:, g % 2, i, :], x1_dram[g * GT + i]), s_g[g % 2 * 4 + i])

        def g_bias(g, i):
            pool.wait(got("gin", g, i), bo_in)
            done["gbo", g, i] = pool.do(lambda e: e.tensor_tensor(x1_g[:, g % 2, i, :], x1_g[:, g % 2, i, :], b_o_sb[:], ALU.add), s_gbo)

        def g_stats(g, i):
            dve.wait(got("gbo", g, i), got("gap", g - 1, GT - 1))
            st = dve.do(lambda e: e.bn_stats(stats[:, i, :], x1_g[:, g % 2, i, :]), s_gst)
            dve.wait(st)
            done["gag", g] = dve.do(lambda e: e.bn_aggr(mean_var[:, i, :], stats[:, i, :]), s_gag)

        def g_rstd(g):
            dve.wait(got("gag", g))
            ve = dve.do(lambda e: e.tensor_scalar(var_eps[:], mean_var[:, :, 1], LN_EPS, None, ALU.add), s_gve)
            pool.wait(ve)
            done["grs", g] = pool.do(lambda e: e.tensor_tensor(rstd[:], var_eps[:], neg_half[:], ALU.pow), s_grs)

        def g_apply(g, i):
            prev = (g, i - 2) if i >= 2 else (g - 1, i + 2)
            dve.wait(got("grs", g), got("gtr", *prev))
            done["gap", g, i] = dve.do(lambda e: e.tensor_scalar(
                x1_n[:, i % 2, :], x1_g[:, g % 2, i, :], mean_var[:, i, 0:1], rstd[:, i:i + 1], ALU.subtract, ALU.mult), s_gap)
            pool.wait(got("gap", g, i), b2_in)
            done["xb", g, i] = pool.do(lambda e: e.tensor_tensor(x1_g[:, g % 2, i, :], x1_g[:, g % 2, i, :], b_2_sb[:], ALU.add), s_xb)

        def g_transpose(g, i):
            pe.wait(got("gap", g, i), got("glo_last"))
            for k in range(KT):
                tr = lambda e, k=k: e.transpose(ps_tr[:, k * P:(k + 1) * P], x1_n[:, i % 2, k * P:(k + 1) * P], ident[:])
                done["gtr", g, i] = pe.do(tr, s_gtr if k == KT - 1 else None)
            src = ps_tr[:].rearrange("p (k t) -> p k t", k=KT)
            hi, lo = [hT[:, g % 2, part, :, i * P:(i + 1) * P] for part in (HI, LO)]
            act.wait(got("gtr", g, i), got("m1", (g - 2) * MT + MT - 1),
                     *((got("w2lo", MT - 1), got("w1lo", MT - 1), got("b1m", MT - 1)) if g == 1 else ()))
            hi_done = act.do(lambda e: e.activation(hi, src, ACT.Copy), s_ghi)
            dve.wait(hi_done)
            done["glo", g, i] = done["glo_last",] = dve.do(lambda e: e.tensor_tensor(lo, src, hi.bitcast(F32), ALU.subtract), s_glo)

        def mlp_up(s):
            g, m = divmod(s, MT)
            pe.wait(got("glo", g, GT - 1), got("w1lo", m), got("gelu", s - 2))
            for k in range(KT):
                for wp, xp in PASSES:
                    first, last = (k, wp, xp) == (0, 0, 0), (k, wp, xp) == (KT - 1,) + PASSES[-1]
                    mm = lambda e, k=k, wp=wp, xp=xp, f=first, l=last: e.matmul(
                        ps_m1[s % 2][:], w_1_sb[:, wp, k, m * P:(m + 1) * P], hT[:, g % 2, xp, k, :], start=f, stop=l)
                    done["m1", s] = pe.do(mm, s_m1 if last else None)
            act.wait(got("m1", s), got("b1", m), got("hlo", s - 2))
            ge = done["gelu", s] = act.do(lambda e: e.activation(gelu[:, s % 2, :], ps_m1[s % 2][:], ACT.Gelu,
                                                                 bias=bias_1[:, m:m + 1]), s_gelu)
            act.wait(ge, got("m2", s - 3))
            hh = act.do(lambda e: e.activation(hid[:, s % 3, HI, :], gelu[:, s % 2, :], ACT.Copy), s_hhi)
            dve.wait(hh)
            done["hlo", s] = dve.do(lambda e: e.tensor_tensor(hid[:, s % 3, LO, :], gelu[:, s % 2, :],
                                                              hid[:, s % 3, HI, :].bitcast(F32), ALU.subtract), s_hlo)

        def mlp_down(s):
            g, m = divmod(s, MT)
            pe.wait(got("hlo", s), got("w2lo", m))
            for i in range(GT):
                if m == 0:
                    pe.wait(got("out", g - 1, i))
                for hp, wp in PASSES:
                    mm = lambda e, i=i, hp=hp, wp=wp: e.matmul(
                        ps_acc[i][:], hid[:, s % 3, hp, i * P:(i + 1) * P], w_2_sb[:, wp, m, :],
                        start=(m == 0 and (hp, wp) == PASSES[0]), stop=(m == MT - 1 and (hp, wp) == PASSES[-1]))
                    done["m2", s] = pe.do(mm, s_m2 if (hp, wp) == PASSES[-1] else None)
                if m == MT - 1:
                    dve.wait(got("m2", s), got("xb", g, i))
                    done["out", g, i] = dve.do(lambda e, i=i: e.tensor_tensor(
                        x1_g[:, g % 2, i, :], ps_acc[i][:], x1_g[:, g % 2, i, :], ALU.add), s_out)
                    sp.wait(got("out", g, i))
                    done["gst", g, i] = sp.do(lambda e, i=i: e.dma_start(out_rows[g * GT + i], x1_g[:, g % 2, i, :]), s_st2[g % 2 * 4 + i])

        g_load(0)
        for m in range(4):
            load_weights(m)
        for i in range(GT):
            g_bias(0, i)
            g_stats(0, i)
        g_rstd(0)
        for i in range(GT):
            g_apply(0, i)
            g_transpose(0, i)
        for m in range(2):
            weight_tile(m)
            load_weights(m + 4)
        for s in range(N_GROUPS * MT + 1):
            g, m = divmod(s, MT)
            if s < N_GROUPS * MT:
                mlp_up(s)
            if g == 0:
                for w in (2 * m + 2, 2 * m + 3):
                    if w < MT:
                        weight_tile(w)
                    if w + 4 < MT:
                        load_weights(w + 4)
            if s >= 1:
                mlp_down(s - 1)
            if g + 1 < N_GROUPS:
                if m == 2:
                    g_load(g + 1)
                if 3 <= m < 7:
                    g_bias(g + 1, m - 3)
                if 4 <= m < 8:
                    g_stats(g + 1, m - 4)
                if m == 8:
                    g_rstd(g + 1)
                if m in (9, 10):
                    g_apply(g + 1, m - 9)
                if 11 <= m < 15:
                    g_transpose(g + 1, m - 11)
                    if m < 13:
                        g_apply(g + 1, m - 9)
        for i in range(GT):
            for g in (N_GROUPS - 2, N_GROUPS - 1):
                sp.wait(got("gst", g, i))

        block = es.enter_context(nc.Block())
        block.sync(lambda e: sp.run(e))
        block.scalar(lambda e: act.run(e))
        block.vector(lambda e: dve.run(e))
        block.gpsimd(lambda e: pool.run(e))
        block.tensor(lambda e: pe.run(e))


def kernel(**inputs):
    import numpy as np
    import concourse.bacc as bacc
    from concourse.bass_utils import run_bass_kernel_spmd

    a = {k.replace("L0_xattn_", ""): np.asarray(v) for k, v in inputs.items()}
    x = a["x"]
    B, L, D = x.shape

    def columns(v):
        return v.reshape(-1, P).T

    lay = {
        "x": x,
        "ctx": a["ctx_1024"],
        "tok_xy": a["fside_BxS2x2_0"].transpose(0, 2, 1),
        "q_xy": a["fside_BxSx2_0"].reshape(-1, P, 2).transpose(1, 0, 2).reshape(P, -1),
        "mask": a["mask_BxS2_bf1"].view(np.uint8),
        "w_qkv": a["in_proj_w"].T,
        "w_o": a["out_proj_w"].T,
        "w_1": a["mlp_w1"].T,
        "w_2": a["mlp_w2"].T,
        "cols": np.concatenate([columns(a[n]) for n in (
            "q_norm_g", "q_norm_b", "kv_norm_g", "kv_norm_b", "in_proj_b", "mlp_norm_g", "mlp_norm_b", "mlp_b1")], axis=1),
        "b_o": a["out_proj_b"].reshape(1, -1),
        "b_2": a["mlp_b2"].reshape(1, -1),
        "sp_scale": a["spatial_scale"].reshape(1, -1),
        "sp_offset": a["spatial_offset"].reshape(1, -1),
    }
    nc = bacc.Bacc("TRN2", target_bir_lowering=False, num_devices=1)
    arrays, aps = {}, []
    for name, v in lay.items():
        arrays[f"in_{name}"] = np.ascontiguousarray(v)
        aps.append(nc.dram_tensor(f"in_{name}", v.shape, mybir.dt.from_np(v.dtype), kind="ExternalInput").ap())
    out = nc.dram_tensor("out_0", x.shape, F32, kind="ExternalOutput").ap()
    x1 = nc.dram_tensor("x1_scratch", (B * L // P, P, D), F32).ap()
    build_block(nc, *aps, out, x1)
    return run_bass_kernel_spmd(nc, [arrays], core_ids=[0]).results[0]["out_0"]
```

```python
from contextlib import ExitStack

import concourse.bass as bass
from concourse import mybir

F32 = mybir.dt.float32
F32R = mybir.dt.float32r
F16 = mybir.dt.float16
U8 = mybir.dt.uint8
ALU = mybir.AluOpType
ACT = mybir.ActivationFunctionType

P = 128
LN_EPS = 1e-05
P_SCALE = 2.0 ** 14
HI, LO = 0, 1
PASSES = ((HI, HI), (HI, LO), (LO, HI))
V_SCALE = 2.0 ** 10
TINY = 1e-30


class Signal:

    def __init__(self, sem, step=1):
        self.sem, self.step, self.count = sem, step, 0


class Queue:

    def __init__(self):
        self.ops, self.seen = [], {}

    def wait(self, *marks):
        for mark in marks:
            if mark is None:
                continue
            signal, value = mark
            if self.seen.get(id(signal), 0) < value:
                self.seen[id(signal)] = value
                self.ops.append(lambda e, s=signal.sem, v=value: e.wait_ge(s, v))

    def do(self, make, signal=None):
        if signal is None:
            self.ops.append(make)
            return None
        signal.count += signal.step
        self.ops.append(lambda e, s=signal: make(e).then_inc(s.sem, s.step))
        return signal, signal.count

    def run(self, engine):
        for op in self.ops:
            op(engine)


def build_block(nc, x, ctx, tok_xy, q_xy, mask, w_qkv, w_o, w_1, w_2, cols, b_o, b_2, sp_scale, sp_offset, out, x1_dram):
    B, L, D = x.shape
    T = ctx.shape[1]
    H = sp_scale.shape[1]
    HD = D // H
    FF = w_1.shape[1]
    KT = D // P
    LC, TC = L // P, T // P
    HG, HPG = H // 4, 4
    MT = FF // P
    N_ITEMS = B * H
    GROUP_TOK = 512
    N_GROUPS = B * L // GROUP_TOK
    GT = GROUP_TOK // P
    SCORE_SCALE = float(HD) ** -0.5
    assert (L, T, D, HD, KT, HG) == (256, 256, 512, 32, 4, 4)

    es = ExitStack()
    with es:
        ARENA, ARENA_END = 16512, 229344
        at, top = {}, [ARENA]

        def sb(name, shape, dt, off=None):
            size = mybir.dt.size(dt)
            for n in shape[1:]:
                size *= n
            if off is None:
                off = top[0]
                top[0] += (size + 31) // 32 * 32
                assert top[0] <= ARENA_END, (name, top[0])
            at[name] = off
            return nc.alloc_sbuf_tensor_at(name, shape, dt, offset=off)

        ident = sb("ident", [P, P], F32)
        cols_sb = sb("cols", [P, cols.shape[1]], F32)
        scale_neg = sb("scale_neg", [P, H], F32)
        offset_sb = sb("offset", [P, H], F32)
        q_neg = sb("q_neg", [P, B * LC * 2], F32)
        gq = sb("gq", [P, KT], F32)
        bias_qkv = sb("bias_qkv", [P, 12], F32)
        neg_half = sb("neg_half", [P, 4], F32)
        stats = sb("stats", [P, 4, 6], F32)
        mean_var = sb("mean_var", [P, 4, 2], F32)
        var_eps = sb("var_eps", [P, 4], F32)
        rstd = sb("rstd", [P, 4], F32)
        b_o_sb = sb("b_o", [P, D], F32)
        SOFT_RING, PT_RING, STACK_RING, DIST_RING = 7, 6, 3, 4
        row_stats = sb("row_stats", [P, 3, SOFT_RING, LC], F32)
        neg_max, row_sum, row_inv = [row_stats[:, i, :, :] for i in range(3)]
        attn_y = sb("attn_y", [P, L], F32)
        x1_t = sb("x1_t", [P, D], F32)

        w_qkv_sb = sb("w_qkv_sb", [P, 2, KT, 3 * D], F32R)
        xT = sb("xT", [P, 2, 2, 2, KT, L], F32R)
        raw = sb("raw", [P, 4, D], F32)
        tok_rows = sb("tok_rows", [P, 2, T], F32)
        sq = sb("sq", [P, LC, T], F32)
        stack = sb("stack", [P, STACK_RING, HPG, 2, L], F32R)
        qk_parts = sb("qk_parts", [P, 3, 2, L], F32R)
        v_scale = sb("v_scale", [P, D], F32)
        soft = sb("soft", [P, SOFT_RING, LC, T], F32)
        pT = sb("pT", [P, PT_RING, 2, TC * L], F16)
        v_parts = sb("v_parts", [P, 2, TC, 2, D], F16)
        dist = sb("dist", [P, DIST_RING, LC, T], F32)
        attnT = sb("attnT", [P, 2, 2, HG, L], F32R)
        w_o_sb = sb("w_o_sb", [P, 2, KT, D], F32R)
        mask_u8 = sb("mask_u8", [P, T], U8)
        mask_row = sb("mask_row", [P, 2, T], F32)

        w_stage = [sb(f"w_stage{i}", [P, KT, D], F32, off) for i, off in enumerate((at["attnT"], at["attnT"] + KT * D * 4, at["pT"]))]
        w_v_square = sb("w_v_square", [P, KT, D], F32R, at["w_o_sb"])
        row_at = at["w_o_sb"] + KT * D * 4
        bias_row = [sb(f"bias_row{i}", [P, D], F32, off) for i, off in enumerate((row_at, row_at + D * 4, at["dist"] + 2 * LC * T * 4))]
        w_v_scaled = sb("w_v_scaled", [P, KT, D], F32, at["w_o_sb"])
        inv_row = sb("inv_row", [P, D], F32, row_at + 2 * D * 4)
        v_norm = sb("v_norm", [P, D], F32, at["pT"] + KT * D * 4)
        bias_w = sb("bias_w", [P, 3 * KT], F32)
        v_inv = sb("v_inv", [P, KT], F32)
        ones = sb("ones", [P, P], F32R)

        CHUNKS, CHUNK = MT // 4, 4
        chunk_bytes = 2 * KT * CHUNK * P * 4
        w_1_sb = [sb(f"w_1_{c}", [P, 2, KT, CHUNK * P], F32R, at["w_qkv_sb"] + c * chunk_bytes) for c in range(CHUNKS)]
        w_2_at = (at["stack"] + chunk_bytes // 2, at["soft"], at["soft"] + chunk_bytes, at["w_o_sb"])
        w_2_sb = [sb(f"w_2_{c}", [P, 2, CHUNK, D], F32R, off) for c, off in enumerate(w_2_at)]
        w_1_raw = [sb(f"w_1_raw{c}", [P, KT, CHUNK * P], F32, at[f"w_1_{c}"] + chunk_bytes // 2) for c in range(CHUNKS)]
        w_2_raw = [sb(f"w_2_raw{c}", [P, CHUNK, D], F32, off + chunk_bytes // 2) for c, off in enumerate(w_2_at)]
        hT = [sb(f"hT{g}", [P, 2, KT, GROUP_TOK], F32R, off)
              for g, off in enumerate((at["w_qkv_sb"] + CHUNKS * chunk_bytes, at["attnT"]))]
        x1_g = [sb(f"x1_g{g}", [P, GT, D], F32, off) for g, off in enumerate((at["raw"], at["soft"] + 2 * chunk_bytes))]
        x1_n = sb("x1_n", [P, 2, D], F32, at["tok_rows"])
        b_2_sb = sb("b_2", [P, D], F32, at["x1_g1"] + GT * D * 4)
        hid_bytes = 2 * GROUP_TOK * 4
        hid = [sb(f"hid{i}", [P, 2, GROUP_TOK], F32R, off)
               for i, off in enumerate((at["stack"], at["stack"] + hid_bytes, at["qk_parts"]))]
        gelu = sb("gelu", [P, 2, GROUP_TOK], F32, at["qk_parts"] + hid_bytes)
        assert at["w_1_0"] + CHUNKS * chunk_bytes + 2 * KT * GROUP_TOK * 4 <= at["raw"] and at["b_2"] + D * 4 <= at["attnT"]
        assert at["w_2_0"] + chunk_bytes <= at["qk_parts"] and at["gelu"] + 2 * GROUP_TOK * 4 <= at["soft"]

        def bank(name):
            return es.enter_context(nc.psum_tensor(name, [P, 512], F32))

        ps_s = [bank("ps_s0"), bank("ps_s1")]
        ps_pt = [bank("ps_pt0"), bank("ps_pt1")]
        ps_pv = bank("ps_pv")
        ps_tr = bank("ps_tr")
        ps_qk = bank("ps_qk")
        ps_vo = bank("ps_vo")

        def sig(name, step=1):
            return Signal(es.enter_context(nc.semaphore(name)), step)

        def dsig(name):
            return sig(name, 16)

        pe, act, dve, pool, sp = Queue(), Queue(), Queue(), Queue(), Queue()

        s_cols, s_small, s_bo = dsig("s_cols"), dsig("s_small"), dsig("s_bo")
        cols_in = sp.do(lambda e: e.dma_start(cols_sb[:], cols), s_cols)
        G_Q, B_Q, G_KV, B_KV, B_IN, G_M, B_M, B_1 = 0, 4, 8, 12, 16, 28, 32, 36

        s_id, s_cst = sig("s_id"), sig("s_cst")
        SMALL = ((scale_neg[:], sp_scale.to_broadcast([P, H])), (offset_sb[:], sp_offset.to_broadcast([P, H])), (q_neg[:], q_xy))
        pool.wait(pool.do(lambda e: e.memset(ident[:], 0.0), s_id))
        ident_done = pool.do(lambda e: e.affine_select(out=ident[:], in_=ident[:], compare_op=ALU.not_equal, fill=1.0,
                                                       base=0, pattern=[[-1, P]], channel_multiplier=1), s_id)
        pool.wait(ident_done)
        ones_done = pool.do(lambda e: e.memset(stack[96:97, :, :, 0, :].bitcast(F32), 1.0), s_id)
        pool.wait(ones_done)
        ones128_done = pool.do(lambda e: e.memset(ones[:].bitcast(F32), 1.0), s_id)
        half_done = pool.do(lambda e: e.memset(neg_half[:], -0.5), s_id)
        dve.wait(cols_in)
        gq_done = dve.do(lambda e: e.tensor_scalar(gq[:], cols_sb[:, G_Q:G_Q + KT], SCORE_SCALE, None, ALU.mult), s_cst)

        s_raw = [dsig(f"s_raw{i}") for i in range(4)]
        s_st, s_ag, s_ve, s_rs, s_ap = sig("s_st"), sig("s_ag"), sig("s_ve"), sig("s_rs"), sig("s_ap")
        s_xtr, s_xhi, s_xlo = sig("s_xtr"), sig("s_xhi"), sig("s_xlo")
        s_qk, s_qkhi, s_qklo = sig("s_qk"), sig("s_qkhi"), sig("s_qklo")
        s_stack = [dsig(f"s_stack{i}") for i in range(4)]
        s_v, s_vhi, s_vlo = sig("s_v"), sig("s_vhi"), sig("s_vlo")
        s_xy, s_sq, s_d2, s_dist = dsig("s_xy"), sig("s_sq"), sig("s_d2"), sig("s_dist")
        s_mu, s_mrow = dsig("s_mu"), sig("s_mrow")
        s_bias, s_score, s_max, s_exp, s_inv, s_norm = [sig(n) for n in ("s_bias", "s_score", "s_max", "s_exp", "s_inv", "s_norm")]
        s_t, s_pthi, s_ptlo, s_pv, s_y, s_ahi, s_alo = [sig(n) for n in ("s_t", "s_pthi", "s_ptlo", "s_pv", "s_y", "s_ahi", "s_alo")]
        s_o, s_res, s_x1 = sig("s_o"), dsig("s_res"), sig("s_x1")
        s_x1st = dsig("s_x1st")
        done = {}
        FIRST_USE = ("xlo_last", "qklo_last", "vo_free", "x1st_last", "gy_last")

        def got(*key):
            if key not in done and (key[0] in FIRST_USE or any(i < 0 for i in key[1:])):
                return None
            return done[key]

        CTX, X = 1, 0
        x_rows = x.rearrange("b (c p) d -> (b c) p d", p=P)
        c_rows = ctx.rearrange("b (c p) d -> (b c) p d", p=P)

        SEC_Q, SEC_K, SEC_V, SEC_O = range(4)
        STAGE = {SEC_Q: 1, SEC_K: 0, SEC_V: 2, SEC_O: 0}
        s_w = [dsig(f"s_w{sec}") for sec in range(4)]
        s_wsq, s_wv, s_vnorm2, s_vsc, s_vroot, s_vinv = sig("s_wsq"), sig("s_wv"), sig("s_vnorm2"), sig("s_vsc"), sig("s_vroot"), dsig("s_vinv")
        s_w_hi, s_w_lo, s_w_lo2 = sig("s_w_hi"), sig("s_w_lo"), sig("s_w_lo2")
        s_brow, s_brow_sb, s_bcol = sig("s_brow"), sig("s_brow_sb"), sig("s_bcol")
        s_bcol_in = [dsig(f"s_bcol_in{sec}") for sec in range(3)]
        ps_brow = {SEC_Q: ps_s[0], SEC_K: ps_s[1], SEC_V: ps_pt[0]}

        def small_load():
            for dst, src in SMALL:
                done["small_in",] = sp.do(lambda e, d=dst, s=src: e.dma_start(d, s), s_small)
            done["bo",] = sp.do(lambda e: e.dma_start(b_o_sb[:], b_o.to_broadcast([P, D])), s_bo)

        def small_negate():
            dve.wait(got("small_in"))
            dve.do(lambda e: e.tensor_scalar(scale_neg[:], scale_neg[:], -1.0, None, ALU.mult), s_cst)
            done["small",] = dve.do(lambda e: e.tensor_scalar(q_neg[:], q_neg[:], -1.0, None, ALU.mult), s_cst)

        def weight_load(sec):
            src = w_o if sec == SEC_O else w_qkv[:, sec * D:(sec + 1) * D]
            sp.wait(*(got("wlo", SEC_K), got("brow", SEC_K)) if sec == SEC_O else ())
            done["win", sec] = sp.do(lambda e: e.dma_start(w_stage[STAGE[sec]][:], src.rearrange("(k p) n -> p k n", p=P)), s_w[sec])

        def weight_bias(sec):
            pe.wait(got("win", sec), cols_in)
            b_ln = B_Q if sec == SEC_Q else B_KV
            for k in range(KT):
                mm = lambda e, k=k: e.matmul(
                    ps_brow[sec][0:1, :], cols_sb[:, b_ln + k:b_ln + k + 1],
                    w_stage[STAGE[sec]][:, k, :].rearrange("p (m q) -> p q m", m=KT), start=(k == 0), stop=(k == KT - 1))
                done["brow", sec] = pe.do(mm, s_brow if k == KT - 1 else None)

        def bias_to_columns(sec):
            act.wait(got("brow", sec))
            row = bias_row[sec][0:1, :]
            copied = act.do(lambda e: e.activation(row, ps_brow[sec][0:1, :], ACT.Copy), s_brow_sb)
            sp.wait(copied)
            done["bcol_in", sec] = sp.do(lambda e: e.dma_start(bias_w[:, sec * KT:(sec + 1) * KT], row), s_bcol_in[sec])

        def bias_column(sec):
            part = slice(sec * KT, (sec + 1) * KT)
            dve.wait(got("bcol_in", sec))
            r = dve.do(lambda e: e.tensor_tensor(bias_qkv[:, part], bias_w[:, part], cols_sb[:, B_IN + sec * KT:B_IN + (sec + 1) * KT], ALU.add), s_bcol)
            if sec == SEC_Q:
                dve.wait(r)
                r = dve.do(lambda e: e.tensor_scalar(bias_qkv[:, part], bias_qkv[:, part], SCORE_SCALE, None, ALU.mult), s_bcol)
            done["bcol", sec] = r

        def weight_split(sec, k):
            raw_w = w_v_scaled[:, k, :] if sec == SEC_V else w_stage[STAGE[sec]][:, k, :]
            hi, lo = [w_o_sb[:, part, k, :] if sec == SEC_O else w_qkv_sb[:, part, k, sec * D:(sec + 1) * D] for part in (HI, LO)]
            act.wait(got("win", sec), gq_done, *(got(*key) for key in (
                ("wlo", SEC_V), ("bcol_in", SEC_K), ("bcol_in", SEC_Q), ("vinv",)) if sec == SEC_O))
            if sec in (SEC_Q, SEC_K):
                g = gq[:, k:k + 1] if sec == SEC_Q else cols_sb[:, G_KV + k:G_KV + k + 1]
                hi_done = act.do(lambda e: e.activation(hi, raw_w, ACT.Copy, scale=g), s_w_hi)
                dve.wait(hi_done)
                done["wlo", sec] = dve.do(lambda e: e.scalar_tensor_tensor(
                    out=lo, in0=raw_w, scalar=g, in1=hi.bitcast(F32), op0=ALU.mult, op1=ALU.subtract), s_w_lo)
            else:
                act.wait(got("wvs", k) if sec == SEC_V else None)
                hi_done = act.do(lambda e: e.activation(hi, raw_w, ACT.Copy), s_w_hi)
                pool.wait(hi_done)
                done["wlo", sec] = pool.do(lambda e: e.tensor_tensor(lo, raw_w, hi.bitcast(F32), ALU.subtract), s_w_lo2)

        def value_square(k):
            act.wait(got("win", SEC_V), cols_in)
            done["wsq", k] = act.do(lambda e: e.activation(
                w_v_square[:, k, :], w_stage[STAGE[SEC_V]][:, k, :], ACT.Square, scale=cols_sb[:, G_KV + k:G_KV + k + 1]), s_wsq)

        def value_norms():
            pe.wait(got("wsq", KT - 1), ones128_done)
            for k in range(KT):
                mm = lambda e, k=k: e.matmul(ps_pt[1][:], ones[:], w_v_square[:, k, :], start=(k == 0), stop=(k == KT - 1))
                done["vnorm2",] = pe.do(mm, s_vnorm2 if k == KT - 1 else None)

        def value_norm_floor():
            dve.wait(got("vnorm2"))
            done["vfloor",] = dve.do(lambda e: e.tensor_scalar(v_norm[:], ps_pt[1][:], TINY, V_SCALE ** -2, ALU.max, ALU.mult), s_vsc)

        def value_norm_root():
            act.wait(got("vfloor"))
            done["vroot",] = act.do(lambda e: e.activation(v_norm[:], v_norm[:], ACT.Sqrt), s_vroot)

        def value_scales():
            dve.wait(got("vroot"))
            done["vscale",] = dve.do(lambda e: e.reciprocal(v_scale[:], v_norm[:]), s_vsc)
            act.wait(got("vroot"))
            row = act.do(lambda e: e.activation(inv_row[0:1, :].rearrange("o (q m) -> o q m", m=KT),
                                                v_norm[0:1, :].rearrange("o (m q) -> o q m", m=KT), ACT.Copy, scale=1.0 / P_SCALE), s_vroot)
            sp.wait(row)
            done["vinv",] = sp.do(lambda e: e.dma_start(v_inv[:], inv_row[0:1, :]), s_vinv)

        def value_scale_weights(k):
            dve.wait(got("wsq", k), got("vnorm2"), got("vscale"))
            done["wvs", k] = dve.do(lambda e: e.scalar_tensor_tensor(
                out=w_v_scaled[:, k, :], in0=w_stage[STAGE[SEC_V]][:, k, :], scalar=cols_sb[:, G_KV + k:G_KV + k + 1],
                in1=v_scale[:], op0=ALU.mult, op1=ALU.mult), s_wv)

        def load_tile(b, i):
            src = (x_rows if i < 2 else c_rows)[b * 2 + i % 2]
            sp.wait(got("xtr", b - 1, i))
            done["raw", b, i] = sp.do(lambda e: e.dma_start(raw[:, i, :], src), s_raw[i])

        def load_coordinates(b):
            sp.wait(got("sq", b - 1))
            done["xy", b] = sp.do(lambda e: e.dma_start(tok_rows[:], tok_xy[b:b + 1].to_broadcast([P, 2, T])), s_xy)

        def load_mask(b):
            sp.wait(got("mrow_conv", b - 1))
            done["mask", b] = sp.do(lambda e: e.dma_start(mask_u8[96:97, :], mask[b:b + 1, :]), s_mu)

        def norm_stats(b, i):
            dve.wait(got("raw", b, i), got("ap", b - 1, i), got("rstd", b - 1, i // 2))
            done["stats", b, i] = dve.do(lambda e: e.bn_stats(stats[:, i, :], raw[:, i, :]), s_st)

        def norm_aggregate(b, i):
            dve.wait(got("stats", b, i))
            done["ag", b, i] = dve.do(lambda e: e.bn_aggr(mean_var[:, i, :], stats[:, i, :]), s_ag)

        def norm_eps(b, which):
            pair = slice(2 * which, 2 * which + 2)
            dve.wait(got("ag", b, 2 * which + 1), got("rstd", b - 1, which))
            done["ve", b, which] = dve.do(lambda e: e.tensor_scalar(
                var_eps[:, pair], mean_var[:, pair, 1], LN_EPS, None, ALU.add), s_ve)

        def norm_rstd(b, which):
            pair = slice(2 * which, 2 * which + 2)
            pool.wait(got("ve", b, which), half_done, got("ap", b - 1, 2 * which + 1))
            done["rstd", b, which] = pool.do(lambda e: e.tensor_tensor(rstd[:, pair], var_eps[:, pair], neg_half[:, pair], ALU.pow), s_rs)

        def norm_apply(b, i):
            dve.wait(got("rstd", b, i // 2), got("ag", b, i))
            done["ap", b, i] = dve.do(lambda e: e.tensor_scalar(
                raw[:, i, :], raw[:, i, :], mean_var[:, i, 0:1], rstd[:, i:i + 1], ALU.subtract, ALU.mult), s_ap)

        def x_transpose(b, i):
            pe.wait(got("ap", b, i), got("xlo_last"), ident_done)
            for k in range(KT):
                tr = lambda e, i=i, k=k: e.transpose(ps_tr[:, k * P:(k + 1) * P], raw[:, i, k * P:(k + 1) * P], ident[:])
                last = pe.do(tr, s_xtr if k == KT - 1 else None)
            done["xtr", b, i] = last

        def x_parts(b, i):
            ring, which, tok = b % 2, i // 2, (i % 2) * P
            src = ps_tr[:].rearrange("p (k t) -> p k t", k=KT)
            hi = xT[:, ring, which, HI, :, tok:tok + P]
            lo = xT[:, ring, which, LO, :, tok:tok + P]
            act.wait(got("xtr", b, i), got("qk", 4 * (b - 2) + 3, 1), got("vproj", b - 2, 1))
            hi_done = act.do(lambda e, o=hi, s=src: e.activation(o, s, ACT.Copy), s_xhi)
            dve.wait(hi_done)
            done["xlo", b, i] = done["xlo_last",] = dve.do(lambda e, o=lo, s=src, h=hi: e.tensor_tensor(
                o, s, h.bitcast(F32), ALU.subtract), s_xlo)

        def qk_steps(G, which):
            b, hg = divmod(G, HG)
            ring = b % 2
            steps = []
            for k in range(KT):
                for wp, xp in PASSES:
                    first, last = (k, wp, xp) == (0, 0, 0), (k, wp, xp) == (KT - 1,) + PASSES[-1]
                    col = which * D + hg * P
                    mm = lambda e, k=k, wp=wp, xp=xp, f=first, l=last, c=col: e.matmul(
                        ps_qk[:, which * L:(which + 1) * L], w_qkv_sb[:, wp, k, c:c + P], xT[:, ring, which, xp, k, :], start=f, stop=l)

                    def step(mm=mm, f=first, l=last):
                        if f:
                            pe.wait(got("xlo", b, 2 * which + 1), got("qklo_last"), got("wlo", SEC_Q), got("wlo", SEC_K))
                        r = pe.do(mm, s_qk if l else None)
                        if l:
                            done["qk", G, which] = r
                    steps.append(step)
            return steps

        def qk_split(G):
            src, col, hi_of, lo_of = [], [], [], []
            for which in range(2):
                src.append(ps_qk[:, which * L:(which + 1) * L])
                col.append(bias_qkv[:, which * KT + G % HG:which * KT + G % HG + 1])
                his = slice(0, 2) if which else slice(1, 3)
                hi_of.append(qk_parts[:, his, which, :])
                lo_of.append(qk_parts[:, 2 if which else 0, which, :])
            act.wait(got("qk", G, 1), got("stack", G - 1), got("bcol", SEC_Q), got("bcol", SEC_K))
            for which in range(2):
                twice = src[which].rearrange("p (o l) -> p o l", o=1).to_broadcast([P, 2, L])
                hi_done = act.do(lambda e, o=hi_of[which], i=twice, c=col[which]: e.activation(o, i, ACT.Identity, bias=c), s_qkhi)
            dve.wait(hi_done)
            for which in range(2):
                done["qklo", G] = done["qklo_last",] = dve.do(
                    lambda e, o=lo_of[which], i=src[which], h=qk_parts[:, 1, which, :], c=col[which]: e.scalar_tensor_tensor(
                        out=o, in0=i, scalar=c, in1=h.bitcast(F32), op0=ALU.add, op1=ALU.subtract), s_qklo)

        def stack_copies(G):
            b, ring = G // HG, G % STACK_RING
            sp.wait(got("qklo", G), got("score", 4 * (G - STACK_RING) + 3), got("mrow", b), ones_done)
            for j in range(HPG):
                src = qk_parts[32 * j:32 * j + 32, :, :, :].bitcast(F32).rearrange("p r w l -> p r (w l)")
                dst = stack[0:96, ring, j, :, :].bitcast(F32).rearrange("p w l -> p (w l)")
                sp.do(lambda e, d=dst, s=src: e.dma_start(d, s), s_stack[ring])
            dst = stack[96:97, ring, :, 1, :].bitcast(F32)
            src = mask_row[96:97, b % 2, :].rearrange("p (o t) -> p o t", o=1).to_broadcast([1, HPG, T])
            done["stack", G] = sp.do(lambda e: e.dma_start(dst, src), s_stack[ring])

        def mask_large(b):
            row, src = mask_row[96:97, b % 2, :], mask_u8[96:97, :]
            dve.wait(got("mask", b), got("stack", 4 * (b - 1) - 1))
            done["mrow_conv", b] = dve.do(lambda e: e.tensor_scalar(row, src, 0.0, -3.0e38, ALU.is_equal, ALU.mult), s_mrow)

        def mask_infinite(b):
            row = mask_row[96:97, b % 2, :]
            dve.wait(got("mrow_conv", b))
            done["mrow", b] = dve.do(lambda e: e.tensor_scalar(row, row, 3.0e38, None, ALU.mult), s_mrow)

        def v_steps(b, tt):
            ring = b % 2
            steps = []
            for k in range(KT):
                for xp, wp in PASSES:
                    first, last = (k, xp, wp) == (0, 0, 0), (k, xp, wp) == (KT - 1,) + PASSES[-1]
                    mm = lambda e, k=k, wp=wp, xp=xp, f=first, l=last: e.matmul(
                        ps_vo[:], xT[:, ring, 1, xp, k, tt * P:(tt + 1) * P], w_qkv_sb[:, wp, k, 2 * D:3 * D], start=f, stop=l)

                    def step(mm=mm, f=first, l=last):
                        if f:
                            pe.wait(got("xlo", b, 3), got("vo_free"), got("wlo", SEC_V))
                        r = pe.do(mm, s_v if l else None)
                        if l:
                            done["vproj", b, tt] = r
                    steps.append(step)
            return steps

        def v_split(b, tt):
            hi, lo = [v_parts[:, b % 2, tt, part, :] for part in (HI, LO)]
            act.wait(got("vproj", b, tt), got("pv", 4 * (b - 2) + 3))
            hi_done = act.do(lambda e: e.activation(hi, ps_vo[:], ACT.Copy), s_vhi)
            dve.wait(hi_done)
            done["v", b, tt] = done["vo_free",] = dve.do(lambda e: e.tensor_tensor(lo, ps_vo[:], hi, ALU.subtract), s_vlo)

        def dist_square(b, c):
            act.wait(got("xy", b), got("small"), got("d2", b - 1), got("bias", H * (b - DIST_RING + 1) - 1))
            if b == 2:
                act.wait(got("bcol_in", SEC_V))
            for lc in range(LC):
                dst = (dist[:, b % DIST_RING, lc, :], sq[:, lc, :])[c]
                col = (b * LC + lc) * 2 + c
                done["sq", b] = act.do(lambda e, o=dst, q=col: e.activation(o, tok_rows[:, c, :], ACT.Square, bias=q_neg[:, q:q + 1]), s_sq)

        def dist_sum(b, lc):
            pool.wait(got("sq", b))
            d = dist[:, b % DIST_RING, lc, :]
            done["d2", b] = done["d2", b, lc] = pool.do(lambda e: e.tensor_tensor(d, d, sq[:, lc, :], ALU.add), s_d2)

        def dist_floor(b, lc):
            pool.wait(got("d2", b, lc))
            d = dist[:, b % DIST_RING, lc, :]
            done["d2max", b] = pool.do(lambda e: e.tensor_scalar(d, d, 0.0, None, ALU.max), s_d2)

        def dist_sqrt(b):
            if b % 2 == 0:
                act.wait(got("d2max", b + 1))
                d = dist[:, b % DIST_RING:b % DIST_RING + 2, :, :]
                done["dist", b] = done["dist", b + 1] = act.do(lambda e: e.activation(d, d, ACT.Sqrt), s_dist)

        def bias_tile(i):
            b, h = divmod(i, H)
            pool.wait(got("dist", b), got("t", i - SOFT_RING), got("small"))
            done["bias", i] = pool.do(lambda e: e.tensor_scalar(
                soft[:, i % SOFT_RING, :, :], dist[:, b % DIST_RING, :, :], scale_neg[:, h:h + 1], offset_sb[:, h:h + 1], ALU.mult, ALU.add), s_bias)

        def scores(i):
            b, h = divmod(i, H)
            ring, j = (i // 4) % STACK_RING, i % 4
            pe.wait(got("stack", i // 4), got("max", i - 2))
            for lc in range(LC):
                mm = lambda e, lc=lc: e.matmul(ps_s[i % 2][:, lc * T:(lc + 1) * T], stack[0:97, ring, j, 0, lc * P:(lc + 1) * P],
                                               stack[0:97, ring, j, 1, :], start=True, stop=True)
                r = pe.do(mm, s_score if lc == LC - 1 else None)
            done["score", i] = r

        def score_max(i):
            dve.wait(got("score", i), got("bias", i), got("exp", i - SOFT_RING))
            for lc in range(LC):
                done["max", i] = done["max", i, lc] = dve.do(lambda e, lc=lc: e.tensor_tensor_reduce(
                    soft[:, i % SOFT_RING, lc, :], ps_s[i % 2][:, lc * T:(lc + 1) * T], soft[:, i % SOFT_RING, lc, :], -1.0, 3.0e38,
                    ALU.add, ALU.min, neg_max[:, i % SOFT_RING, lc:lc + 1]), s_max)

        def exps(i):
            act.wait(got("inv", i - SOFT_RING))
            for lc in range(LC):
                act.wait(got("max", i, lc))
                done["exp", i] = act.do(lambda e, lc=lc: e.activation(
                    soft[:, i % SOFT_RING, lc, :], soft[:, i % SOFT_RING, lc, :], ACT.Exp, scale=-1.0, bias=neg_max[:, i % SOFT_RING, lc:lc + 1],
                    accum_out=row_sum[:, i % SOFT_RING, lc:lc + 1]), s_exp)

        def inverse(i):
            dve.wait(got("exp", i), got("norm", i - SOFT_RING))
            done["inv", i] = dve.do(lambda e: e.reciprocal(row_inv[:, i % SOFT_RING, :], row_sum[:, i % SOFT_RING, :]), s_inv)

        def normalise(i):
            pool.wait(got("inv", i))
            for lc in range(LC):
                done["norm", i] = pool.do(lambda e, lc=lc: e.tensor_scalar(
                    soft[:, i % SOFT_RING, lc, :], soft[:, i % SOFT_RING, lc, :], row_inv[:, i % SOFT_RING, lc:lc + 1], P_SCALE, ALU.mult, ALU.mult), s_norm)

        def p_transpose(i):
            pe.wait(got("norm", i), got("ptlo", i - 2))
            for tc in range(TC):
                for lc in range(LC):
                    tr = lambda e, tc=tc, lc=lc: e.transpose(
                        ps_pt[i % 2][:, tc * L + lc * P:tc * L + (lc + 1) * P], soft[:, i % SOFT_RING, lc, tc * P:(tc + 1) * P], ident[:])
                    r = pe.do(tr, s_t if (tc, lc) == (TC - 1, LC - 1) else None)
            done["t", i] = r

        def p_parts(i):
            hi, lo = pT[:, i % PT_RING, 0, :], pT[:, i % PT_RING, 1, :]
            act.wait(got("t", i), got("pv", (i - PT_RING) // 4) if i >= PT_RING else None)
            hi_done = act.do(lambda e: e.activation(hi, ps_pt[i % 2][:], ACT.Copy), s_pthi)
            dve.wait(hi_done)
            done["ptlo", i] = dve.do(lambda e: e.tensor_tensor(lo, ps_pt[i % 2][:], hi, ALU.subtract), s_ptlo)

        ROUNDS = [(tc, pp, vp) for tc in range(TC) for pp, vp in PASSES]

        def attend(G):
            b, hg = divmod(G, HG)
            pe.wait(got("ptlo", 4 * G + 3), got("v", b, 1), got("y", G - 1))
            for n, (tc, pp, vp) in enumerate(ROUNDS):
                for j in range(HPG):
                    h = hg * HPG + j
                    mm = lambda e, tc=tc, pp=pp, vp=vp, j=j, h=h, n=n: e.matmul(
                        ps_pv[32 * j:32 * j + 32, 0:L], v_parts[:, b % 2, tc, vp, h * HD:(h + 1) * HD],
                        pT[:, (4 * G + j) % PT_RING, pp, tc * L:(tc + 1) * L], start=(n == 0), stop=(n == len(ROUNDS) - 1))
                    r = pe.do(mm, s_pv if (n, j) == (len(ROUNDS) - 1, HPG - 1) else None)
            done["pv", G] = r

        def attn_scale(G):
            hg = G % HG
            dve.wait(got("pv", G), got("alo", G - 1), got("bcol", SEC_V), got("vinv"))
            done["y", G] = dve.do(lambda e: e.tensor_scalar(
                attn_y[:], ps_pv[:, 0:L], v_inv[:, hg:hg + 1], bias_qkv[:, 2 * KT + hg:2 * KT + hg + 1], ALU.mult, ALU.add), s_y)

        def attn_hi(G):
            b, hg = divmod(G, HG)
            act.wait(got("y", G), got("oproj", b - 2, 1))
            done["ahi", G] = act.do(lambda e: e.activation(attnT[:, b % 2, HI, hg, :], attn_y[:], ACT.Copy), s_ahi)

        def attn_lo(G):
            b, hg = divmod(G, HG)
            pool.wait(got("ahi", G))
            done["alo", G] = pool.do(lambda e: e.tensor_tensor(
                attnT[:, b % 2, LO, hg, :], attn_y[:], attnT[:, b % 2, HI, hg, :].bitcast(F32), ALU.subtract), s_alo)

        def o_steps(b, tt):
            steps = []
            for k in range(KT):
                for ap_, wp in PASSES:
                    first, last = (k, ap_, wp) == (0, 0, 0), (k, ap_, wp) == (KT - 1,) + PASSES[-1]
                    mm = lambda e, k=k, wp=wp, ap_=ap_, f=first, l=last: e.matmul(
                        ps_vo[:], attnT[:, b % 2, ap_, k, tt * P:(tt + 1) * P], w_o_sb[:, wp, k, :], start=f, stop=l)

                    def step(mm=mm, f=first, l=last):
                        if f:
                            pe.wait(got("alo", 4 * b + 3), got("vo_free"), got("wlo", SEC_O))
                        r = pe.do(mm, s_o if l else None)
                        if l:
                            done["oproj", b, tt] = r
                    steps.append(step)
            return steps

        def load_residual(b, tt):
            sp.wait(got("x1st_last"))
            done["res", b, tt] = sp.do(lambda e: e.dma_start(x1_t[:], x_rows[b * 2 + tt]), s_res)

        def add_residual(b, tt):
            dve.wait(got("oproj", b, tt), got("res", b, tt))
            r = done["vo_free",] = dve.do(lambda e: e.tensor_tensor(x1_t[:], ps_vo[:], x1_t[:], ALU.add), s_x1)
            sp.wait(r)
            done["x1st", b, tt] = done["x1st_last",] = sp.do(lambda e: e.dma_start(x1_dram[b * 2 + tt], x1_t[:]), s_x1st)

        s_w1, s_w2 = [dsig(f"s_w1_{c}") for c in range(CHUNKS)], [dsig(f"s_w2_{c}") for c in range(CHUNKS)]
        s_w1hi, s_w1lo, s_w2hi, s_w2lo, s_b2 = sig("s_w1hi"), sig("s_w1lo"), sig("s_w2hi"), sig("s_w2lo"), dsig("s_b2")
        s_g = [dsig(f"s_g{i}") for i in range(2 * GT)]
        s_gbo, s_gst, s_gag, s_gve, s_grs, s_gap = [sig(n) for n in ("s_gbo", "s_gst", "s_gag", "s_gve", "s_grs", "s_gap")]
        s_gtr, s_gy, s_ghi, s_glo = [sig(n) for n in ("s_gtr", "s_gy", "s_ghi", "s_glo")]
        s_m1, s_gelu, s_hhi, s_hlo, s_m2, s_xb, s_out = [sig(n) for n in ("s_m1", "s_gelu", "s_hhi", "s_hlo", "s_m2", "s_xb", "s_out")]
        s_st2 = [dsig(f"s_st2_{i}") for i in range(2 * GT)]
        ps_acc = [ps_s[0], ps_s[1], ps_pt[0], ps_pt[1]]
        ps_m1 = [ps_qk, ps_tr]
        out_rows = out.rearrange("b (c p) d -> (b c) p d", p=P)
        LAST_G, LAST_B, LAST_I = B * HG - 1, B - 1, B * H - 1

        def w1_load(c):
            sp.wait(got("qk", LAST_G, 1), got("vproj", LAST_B, 1))
            done["w1in", c] = sp.do(lambda e: e.dma_start(
                w_1_raw[c][:],
                w_1[:, c * CHUNK * P:(c + 1) * CHUNK * P].rearrange("(k p) n -> p k n", p=P)), s_w1[c])

        def w1_hi(c, k):
            act.wait(got("w1in", c))
            done["w1hi", c, k] = act.do(lambda e: e.activation(
                w_1_sb[c][:, HI, k, :], w_1_raw[c][:, k, :], ACT.Copy), s_w1hi)

        def w1_lo(c, k):
            dve.wait(got("w1hi", c, k))
            done["w1lo", c] = dve.do(lambda e: e.tensor_tensor(
                w_1_sb[c][:, LO, k, :], w_1_raw[c][:, k, :], w_1_sb[c][:, HI, k, :].bitcast(F32), ALU.subtract), s_w1lo)

        def w2_load(c):
            sp.wait(got(*(("score", LAST_I - HPG), ("pv", LAST_G), ("pv", LAST_G), ("oproj", LAST_B, 1))[c]))
            done["w2in", c] = sp.do(lambda e: e.dma_start(
                w_2_raw[c][:],
                w_2[c * CHUNK * P:(c + 1) * CHUNK * P, :].rearrange("(m p) n -> p m n", p=P)), s_w2[c])

        def w2_split(m):
            c, i = divmod(m, CHUNK)
            hi, lo = [w_2_sb[c][:, part, i, :] for part in (HI, LO)]
            raw_w = w_2_raw[c][:, i, :]
            act.wait(got("w2in", c))
            hi_done = act.do(lambda e: e.activation(hi, raw_w, ACT.Copy), s_w2hi)
            dve.wait(hi_done)
            done["w2lo", m] = dve.do(lambda e: e.tensor_tensor(lo, raw_w, hi.bitcast(F32), ALU.subtract), s_w2lo)

        def b2_load():
            sp.wait(got("bias", LAST_I))
            done["b2in",] = sp.do(lambda e: e.dma_start(b_2_sb[:], b_2.to_broadcast([P, D])), s_b2)

        def g_load(g):
            for i in range(GT):
                sp.wait(*[got("x1st", 2 * g + 1, tt) for tt in range(2)], got("gst", g - 2, i),
                        *(got("xtr", LAST_B, n) for n in range(4)) if g == 0 else (got("pv", LAST_G), got("bias", LAST_I)))
                done["gin", g, i] = sp.do(lambda e, i=i: e.dma_start(x1_g[g % 2][:, i, :], x1_dram[g * GT + i]), s_g[g % 2 * 4 + i])

        def g_bias(g, i):
            pool.wait(got("gin", g, i), got("bo"))
            tile = x1_g[g % 2][:, i, :]
            done["gbo", g, i] = pool.do(lambda e: e.tensor_tensor(tile, tile, b_o_sb[:], ALU.add), s_gbo)

        def g_stats(g, i):
            dve.wait(got("gbo", g, i), *(got("gap", g - 1, n) for n in range(GT)), *(got("ap", LAST_B, n) for n in range(4)))
            st = dve.do(lambda e: e.bn_stats(stats[:, i, :], x1_g[g % 2][:, i, :]), s_gst)
            dve.wait(st)
            done["gag", g] = dve.do(lambda e: e.bn_aggr(mean_var[:, i, :], stats[:, i, :]), s_gag)

        def g_eps(g):
            dve.wait(got("gag", g), got("rstd", LAST_B, CTX), got("rstd", LAST_B, X))
            done["gve", g] = dve.do(lambda e: e.tensor_scalar(var_eps[:], mean_var[:, :, 1], LN_EPS, None, ALU.add), s_gve)

        def g_rstd(g):
            pool.wait(got("gve", g))
            done["grs", g] = pool.do(lambda e: e.tensor_tensor(rstd[:], var_eps[:], neg_half[:], ALU.pow), s_grs)

        def g_apply(g, i):
            prev = (g, i - 2) if i >= 2 else (g - 1, i + 2)
            dve.wait(got("grs", g), got("glo", *prev), got("sq", LAST_B), got("d2", LAST_B))
            done["gap", g, i] = dve.do(lambda e: e.tensor_scalar(
                x1_n[:, i % 2, :], x1_g[g % 2][:, i, :], mean_var[:, i, 0:1], rstd[:, i:i + 1], ALU.subtract, ALU.mult), s_gap)

        def g_transpose(g, i):
            bank = ps_tr if g == 0 else ps_pv
            pe.wait(got("gap", g, i), got("gy_last"), got("xlo_last"), got("y", LAST_G) if g else None)
            for k in range(KT):
                tr = lambda e, k=k: e.transpose(bank[:, k * P:(k + 1) * P], x1_n[:, i % 2, k * P:(k + 1) * P], ident[:])
                done["gtr", g, i] = pe.do(tr, s_gtr if k == KT - 1 else None)

        def g_affine(g, i):
            bank = ps_tr if g == 0 else ps_pv
            dve.wait(got("gtr", g, i))
            for k in range(KT):
                done["gy", g, i] = done["gy_last",] = dve.do(lambda e, k=k: e.tensor_scalar(
                    x1_n[:, i % 2, k * P:(k + 1) * P], bank[:, k * P:(k + 1) * P],
                    cols_sb[:, G_M + k:G_M + k + 1], cols_sb[:, B_M + k:B_M + k + 1], ALU.mult, ALU.add), s_gy)

        def g_parts(g, i):
            src = x1_n[:, i % 2, :].rearrange("p (k t) -> p k t", k=KT)
            hi, lo = [hT[g % 2][:, part, :, i * P:(i + 1) * P] for part in (HI, LO)]
            act.wait(got("gy", g, i), got("m1", (g - 2) * MT + MT - 1),
                     *((got("qk", LAST_G, 1), got("vproj", LAST_B, 1)) if g == 0 else (got("oproj", LAST_B, 1),)))
            hi_done = act.do(lambda e: e.activation(hi, src, ACT.Copy), s_ghi)
            pool.wait(hi_done)
            done["glo", g, i] = pool.do(lambda e: e.tensor_tensor(lo, src, hi.bitcast(F32), ALU.subtract), s_glo)

        def g_bias2(g, i):
            pool.wait(got("gap", g, i), got("b2in"))
            tile = x1_g[g % 2][:, i, :]
            done["xb", g, i] = pool.do(lambda e: e.tensor_tensor(tile, tile, b_2_sb[:], ALU.add), s_xb)

        def mlp_up(s):
            g, m = divmod(s, MT)
            pe.wait(got("glo", g, GT - 1), got("w1lo", m // CHUNK), got("gelu", s - 2), got("qklo_last"), got("gy", 0, GT - 1))
            for k in range(KT):
                for wp, xp in PASSES:
                    first, last = (k, wp, xp) == (0, 0, 0), (k, wp, xp) == (KT - 1,) + PASSES[-1]
                    mm = lambda e, k=k, wp=wp, xp=xp, f=first, l=last: e.matmul(
                        ps_m1[s % 2][:], w_1_sb[m // CHUNK][:, wp, k, m % CHUNK * P:(m % CHUNK + 1) * P],
                        hT[g % 2][:, xp, k, :], start=f, stop=l)
                    done["m1", s] = pe.do(mm, s_m1 if last else None)

        def mlp_gelu(s):
            m = s % MT
            act.wait(got("m1", s), got("hlo", s - 2), got("score", LAST_I), got("stack", LAST_G))
            ge = done["gelu", s] = act.do(lambda e: e.activation(gelu[:, s % 2, :], ps_m1[s % 2][:], ACT.Gelu,
                                                                 bias=cols_sb[:, B_1 + m:B_1 + m + 1]), s_gelu)
            act.wait(ge, got("m2", s - 3))
            hh = act.do(lambda e: e.activation(hid[s % 3][:, HI, :], gelu[:, s % 2, :], ACT.Copy), s_hhi)
            dve.wait(hh)
            done["hlo", s] = dve.do(lambda e: e.tensor_tensor(
                hid[s % 3][:, LO, :], gelu[:, s % 2, :], hid[s % 3][:, HI, :].bitcast(F32), ALU.subtract), s_hlo)

        def mlp_down(s):
            g, m = divmod(s, MT)
            pe.wait(got("hlo", s), got("w2lo", m), got("max", LAST_I), got("ptlo", LAST_I))
            for i in range(GT):
                if m == 0:
                    pe.wait(got("out", g - 1, i))
                for hp, wp in PASSES:
                    mm = lambda e, i=i, hp=hp, wp=wp: e.matmul(
                        ps_acc[i][:], hid[s % 3][:, hp, i * P:(i + 1) * P], w_2_sb[m // CHUNK][:, wp, m % CHUNK, :],
                        start=(m == 0 and (hp, wp) == PASSES[0]), stop=(m == MT - 1 and (hp, wp) == PASSES[-1]))
                    done["m2", s] = pe.do(mm, s_m2 if (hp, wp) == PASSES[-1] else None)
                if m == MT - 1:
                    tile = x1_g[g % 2][:, i, :]
                    dve.wait(got("m2", s), got("xb", g, i))
                    done["out", g, i] = dve.do(lambda e, i=i, t=tile: e.tensor_tensor(t, ps_acc[i][:], t, ALU.add), s_out)
                    sp.wait(got("out", g, i))
                    done["gst", g, i] = sp.do(lambda e, i=i, t=tile: e.dma_start(out_rows[g * GT + i], t), s_st2[g % 2 * 4 + i])

        def mlp_side(s):
            g, m = divmod(s, MT)
            if g == 0:
                for c, first in ((2, 5), (3, 9)):
                    for k in (2 * (m - first), 2 * (m - first) + 1):
                        if 0 <= k < KT:
                            w1_hi(c, k)
                            w1_lo(c, k)
                if CHUNK < m:
                    w2_split(m - 1)
            if g == 1 and m == 0:
                w2_split(MT - 1)
            if 8 <= m < 12:
                g_bias2(g, m - 8)
            if g + 1 < N_GROUPS:
                if m == 4:
                    g_load(g + 1)
                if m in (6, 7):
                    g_bias(g + 1, 2 * (m - 6))
                    g_bias(g + 1, 2 * (m - 6) + 1)
                if m in (7, 8):
                    g_stats(g + 1, 2 * (m - 7))
                    g_stats(g + 1, 2 * (m - 7) + 1)
                if m == 9:
                    g_eps(g + 1)
                    g_rstd(g + 1)
                if m == 10:
                    g_apply(g + 1, 0)
                    g_apply(g + 1, 1)
                if 12 <= m < 14:
                    g_apply(g + 1, m - 10)
                if 11 <= m < 15:
                    g_transpose(g + 1, m - 11)
                    g_affine(g + 1, m - 11)
                    g_parts(g + 1, m - 11)

        def mlp_step(q):
            s, second = divmod(q, 2)
            if second:
                if 0 <= s - 2:
                    mlp_down(s - 2)
            elif s < N_GROUPS * MT:
                mlp_up(s)
                mlp_gelu(s)
                mlp_side(s)

        fill_vo, fill_qk = [], []
        ITEM, GROUP, BATCH = 1, HPG, H

        def v_fill(b, tt):
            fill_vo.extend(v_steps(b, tt))

        def fill(queue, n):
            for step in queue[:n]:
                step()
            del queue[:n]

        TILES = (2, 3, 0, 1)

        def tiles(first, step):
            return [(BATCH, first + 4 * n, lambda b, i=i: step(b, i)) for n, i in enumerate(TILES)]

        def halves(first, step, apart=4):
            return [(BATCH, first + apart * n, lambda b, n=n: step(b, n)) for n in range(2)]

        def v_halves(first, step):
            return [(BATCH, first + 4 * n, lambda b, n=n: step(b, n) if b else None) for n in range(2)]

        schedule = [
            (ITEM, -1, scores),
            (ITEM, 0, score_max),
            (ITEM, 2, inverse),
            (ITEM, 5, p_parts),
            (GROUP, -7, qk_split),
            (GROUP, -7, stack_copies),
            *v_halves(-10, v_split),
            *halves(30, add_residual),
            *tiles(-25, x_parts),
            (GROUP, 11, attn_scale),
            (ITEM, 1, exps),
            (GROUP, 12, attn_hi),
            *tiles(-36, norm_stats),
            (BATCH, -29, lambda b: norm_rstd(b, CTX)),
            (BATCH, -21, lambda b: norm_rstd(b, X)),
            *tiles(-28, norm_apply),
            *tiles(-36, norm_aggregate),
            (BATCH, -31, lambda b: norm_eps(b, CTX)),
            (BATCH, -23, lambda b: norm_eps(b, X)),
            *halves(-28, dist_square),
            (BATCH, -10, mask_large),
            (BATCH, -9, mask_infinite),
            *halves(-23, dist_sum, 2),
            *halves(-20, dist_floor, 1),
            (BATCH, -2, dist_sqrt),
            (ITEM, 3, normalise),
            (ITEM, -1, bias_tile),
            (GROUP, 13, attn_lo),
            (ITEM, 4, p_transpose),
            (GROUP, 9, attend),
            (GROUP, -10, lambda G: fill_qk.extend(qk_steps(G, 0) + qk_steps(G, 1))),
            *v_halves(-13, v_fill),
            *halves(27, lambda b, tt: fill_vo.extend(o_steps(b, tt))),
            *tiles(-26, x_transpose),
            *tiles(-41, load_tile),
            (BATCH, -33, load_coordinates),
            (BATCH, -17, load_mask),
            (BATCH, 20, lambda b: load_residual(b, 0)),
            (BATCH, 30, lambda b: load_residual(b, 1)),
        ]
        QK_FILL, VO_FILL = (6, 0, 12, 6), (5, 2, 0, 5)
        single = {}

        def once(slot, step, *args):
            single.setdefault(slot, []).append((step, args))

        FIRST_SLOT = -41
        once(-29, weight_load, SEC_K)
        once(-28, weight_load, SEC_Q)
        once(-31, small_load)
        once(-27, weight_load, SEC_V)
        once(-12, weight_load, SEC_O)
        once(-29, small_negate)
        for slot, sec in ((-22, SEC_K), (-14, SEC_Q), (1, SEC_V)):
            once(slot, weight_bias, sec)
            once(max(slot + 1, -13), bias_to_columns, sec)
            once(max(slot + 6, -8), bias_column, sec)
        once(-16, value_norms)
        once(-15, value_norm_floor)
        once(-14, value_norm_root)
        once(-13, value_scales)
        for k in range(KT):
            once(-24 + k, weight_split, SEC_K, k)
            once(-20 + k, weight_split, SEC_Q, k)
            once(-20 + k, value_square, k)
            once(-10 + k, value_scale_weights, k)
            once(-9 + k, weight_split, SEC_V, k)
            once(-4 + k, weight_split, SEC_O, k)
        for tt in range(TC):
            for slot, step in ((-5, v_fill), (-2, v_split)):
                once(slot + 4 * tt, step, 0, tt)

        once(N_ITEMS - 28, g_load, 0)
        for i in range(GT):
            once(N_ITEMS - 24 + i, g_bias, 0, i)
            once(N_ITEMS - 23 + i, g_stats, 0, i)
        once(N_ITEMS - 19, g_eps, 0)
        once(N_ITEMS - 18, g_rstd, 0)
        for i in range(GT):
            once(N_ITEMS + (-17, -16, -9, -7)[i], g_apply, 0, i)
            once(N_ITEMS - 12 + 2 * i, g_transpose, 0, i)
            once(N_ITEMS - 11 + 2 * i, g_affine, 0, i)
            once(N_ITEMS - 10 + 2 * i, g_parts, 0, i)
        for c in range(CHUNKS):
            once(N_ITEMS - 11 + 2 * c, w1_load, c)
        for k in range(KT):
            for c in range(2):
                once(N_ITEMS - 7 + KT * c + k, w1_hi, c, k)
                once(N_ITEMS - 6 + KT * c + k, w1_lo, c, k)
        once(N_ITEMS - 4, w2_load, 0)
        for m in range(CHUNK):
            once(N_ITEMS + 1 + m, w2_split, m)
        once(N_ITEMS - 2, mlp_up, 0)
        once(N_ITEMS - 1, mlp_up, 1)
        once(N_ITEMS + 2, mlp_gelu, 0)
        once(N_ITEMS + 2, mlp_gelu, 1)
        once(N_ITEMS + 3, mlp_up, 2)
        once(N_ITEMS + 3, mlp_gelu, 2)
        once(N_ITEMS + 6, w2_load, 1)
        once(N_ITEMS + 6, w2_load, 2)
        once(N_ITEMS + 6, b2_load)
        once(N_ITEMS + 18, w2_load, 3)
        FIRST_MLP_SLOT, FIRST_MLP_STEP = 5, 5
        LAST_SLOT = N_ITEMS - H + 35
        for slot in range(FIRST_SLOT, LAST_SLOT):
            for every, first, step in schedule:
                k, rest = divmod(slot - first, every)
                if rest == 0 and 0 <= k < N_ITEMS // every:
                    step(k)
            for step, args in single.get(slot, ()):
                step(*args)
            fill(fill_qk, QK_FILL[slot % HPG])
            fill(fill_vo, VO_FILL[slot % HPG])
            if slot >= N_ITEMS + FIRST_MLP_SLOT:
                mlp_step(FIRST_MLP_STEP + slot - N_ITEMS - FIRST_MLP_SLOT)

        for q in range(FIRST_MLP_STEP + LAST_SLOT - N_ITEMS - FIRST_MLP_SLOT, 2 * (N_GROUPS * MT + 2)):
            mlp_step(q)
        for i in range(GT):
            for g in (N_GROUPS - 2, N_GROUPS - 1):
                sp.wait(got("gst", g, i))

        block = es.enter_context(nc.Block())
        block.sync(lambda e: sp.run(e))
        block.scalar(lambda e: act.run(e))
        block.vector(lambda e: dve.run(e))
        block.gpsimd(lambda e: pool.run(e))
        block.tensor(lambda e: pe.run(e))


def kernel(**inputs):
    import numpy as np
    import concourse.bacc as bacc
    from concourse.bass_utils import run_bass_kernel_spmd

    a = {k.replace("L0_xattn_", ""): np.asarray(v) for k, v in inputs.items()}
    x = a["x"]
    B, L, D = x.shape

    def columns(v):
        return v.reshape(-1, P).T

    lay = {
        "x": x,
        "ctx": a["ctx_1024"],
        "tok_xy": a["fside_BxS2x2_0"].transpose(0, 2, 1),
        "q_xy": a["fside_BxSx2_0"].reshape(-1, P, 2).transpose(1, 0, 2).reshape(P, -1),
        "mask": a["mask_BxS2_bf1"].view(np.uint8),
        "w_qkv": a["in_proj_w"].T,
        "w_o": a["out_proj_w"].T,
        "w_1": a["mlp_w1"].T,
        "w_2": a["mlp_w2"].T,
        "cols": np.concatenate([columns(a[n]) for n in (
            "q_norm_g", "q_norm_b", "kv_norm_g", "kv_norm_b", "in_proj_b", "mlp_norm_g", "mlp_norm_b", "mlp_b1")], axis=1),
        "b_o": a["out_proj_b"].reshape(1, -1),
        "b_2": a["mlp_b2"].reshape(1, -1),
        "sp_scale": a["spatial_scale"].reshape(1, -1),
        "sp_offset": a["spatial_offset"].reshape(1, -1),
    }
    nc = bacc.Bacc("TRN2", target_bir_lowering=False, num_devices=1)
    arrays, aps = {}, []
    for name, v in lay.items():
        arrays[f"in_{name}"] = np.ascontiguousarray(v)
        aps.append(nc.dram_tensor(f"in_{name}", v.shape, mybir.dt.from_np(v.dtype), kind="ExternalInput").ap())
    out = nc.dram_tensor("out_0", x.shape, F32, kind="ExternalOutput").ap()
    x1 = nc.dram_tensor("x1_scratch", (B * L // P, P, D), F32).ap()
    build_block(nc, *aps, out, x1)
    return run_bass_kernel_spmd(nc, [arrays], core_ids=[0]).results[0]["out_0"]
```
